# Optimizing a Trainium2 kernel written in Bass

```python
import numpy as np
import jax
import jax.numpy as jnp

def _softmax(x, axis=-1):
    return jax.nn.softmax(x, axis=axis)

def _gelu(x):
    return jax.nn.gelu(x, approximate=True)

def _silu(x):
    return jax.nn.silu(x)

def _sigmoid(x):
    return jax.nn.sigmoid(x)

def _layernorm(x, axis=-1, eps=1e-05):
    m = jnp.mean(x, axis=axis, keepdims=True)
    v = jnp.var(x, axis=axis, keepdims=True)
    return (x - m) / jnp.sqrt(v + eps)

def _scatter_add(tgt, idx, src, axis=0):
    return tgt.at[idx].add(src)

def _segment_sum(src, seg, n):
    return jax.ops.segment_sum(src, seg, n)
kernel_name = 'mk_prb_d1_jaxref_r8_3da866'

def setup_inputs(seed: int=0):
    np.random.seed(seed)
    _w = jnp.asarray

    def _L0_attn_setup():
        import math
        import jax, jax.numpy as jnp
        import numpy as np
        L, D, H, F = (4, 128, 16, 512)
        HD = D // H
        EPS = 1e-05

        def get_alibi_slopes(num_heads):
            closest = 2 ** math.floor(math.log2(num_heads))
            base = 2 ** (-2 ** (-(math.log2(closest) - 3)))
            slopes = base ** np.arange(1, closest + 1)
            if closest != num_heads:
                extra_base = 2 ** (-2 ** (-(math.log2(2 * closest) - 3)))
                extra = extra_base ** np.arange(1, 2 * (num_heads - closest) + 1, 2)
                slopes = np.concatenate([slopes, extra])
            return jnp.asarray(slopes, dtype=jnp.float32)

        def build_mask(num_heads, T):
            pos = jnp.arange(T)
            dist = pos[None, :] - pos[:, None]
            alibi = get_alibi_slopes(num_heads)[:, None, None] * dist[None]
            causal = jnp.where(dist > 0, -jnp.inf, 0.0).astype(jnp.float32)
            return causal[None] + alibi

        def layer_norm(x, w, b):
            mu = jnp.mean(x, axis=-1, keepdims=True)
            var = jnp.mean(jnp.square(x - mu), axis=-1, keepdims=True)
            return (x - mu) * jax.lax.rsqrt(var + EPS) * w + b

        def mha(x, mask, Wi, bi, Wo, bo):
            B, T, _ = x.shape
            qkv = x @ Wi.T + bi
            q, k, v = jnp.split(qkv, 3, axis=-1)
            q = q.reshape(B, T, H, HD).transpose(0, 2, 1, 3)
            k = k.reshape(B, T, H, HD).transpose(0, 2, 1, 3)
            v = v.reshape(B, T, H, HD).transpose(0, 2, 1, 3)
            scores = jnp.einsum('bhqd,bhkd->bhqk', q, k) / math.sqrt(HD)
            scores = scores + mask[None]
            attn = jax.nn.softmax(scores, axis=-1)
            out = jnp.einsum('bhqk,bhkd->bhqd', attn, v)
            out = out.transpose(0, 2, 1, 3).reshape(B, T, D)
            return out @ Wo.T + bo
        key = jax.random.key(seed)
        ks = jax.random.split(key, 13)
        s = 0.02
        inp = {'x': jax.random.normal(ks[0], (2, 256, D), dtype=jnp.float32), 'in_proj_w': jax.random.normal(ks[1], (L, 3 * D, D), dtype=jnp.float32) * s, 'in_proj_b': jnp.zeros((L, 3 * D), dtype=jnp.float32), 'out_proj_w': jax.random.normal(ks[2], (L, D, D), dtype=jnp.float32) * s, 'out_proj_b': jnp.zeros((L, D), dtype=jnp.float32), 'ffn1_w': jax.random.normal(ks[3], (L, F, D), dtype=jnp.float32) * s, 'ffn1_b': jnp.zeros((L, F), dtype=jnp.float32), 'ffn2_w': jax.random.normal(ks[4], (L, D, F), dtype=jnp.float32) * s, 'ffn2_b': jnp.zeros((L, D), dtype=jnp.float32), 'ln1_w': jnp.ones((L, D), dtype=jnp.float32), 'ln1_b': jnp.zeros((L, D), dtype=jnp.float32), 'ln2_w': jnp.ones((L, D), dtype=jnp.float32), 'ln2_b': jnp.zeros((L, D), dtype=jnp.float32), 'final_w': jnp.ones((D,), dtype=jnp.float32), 'final_b': jnp.zeros((D,), dtype=jnp.float32)}
        return inp
    _L0_attn_in = _L0_attn_setup()

    def _L0_ffn_setup():
        import jax, jax.numpy as jnp
        import numpy as np
        B, T, D, E, H = (4, 256, 128, 4, 8)
        EPS = 1e-05

        def _uniform(k, shape, bound):
            return jax.random.uniform(k, shape, jnp.float32, -bound, bound)

        def _layernorm(x, w, b):
            mu = jnp.mean(x, axis=-1, keepdims=True)
            var = jnp.mean(jnp.square(x - mu), axis=-1, keepdims=True)
            return (x - mu) * jax.lax.rsqrt(var + EPS) * w + b
        key = jax.random.key(seed)
        ks = jax.random.split(key, 12)
        wb = np.sqrt(6.0 / D) / np.sqrt(6.0)
        wb = 1.0 / np.sqrt(D)
        return {'x': jax.random.normal(ks[0], (B, T, D), jnp.float32), 'router_prob': jax.random.uniform(ks[1], (B, T, E), jnp.float32), 'norm_w': jnp.ones((D,), jnp.float32), 'norm_b': jnp.zeros((D,), jnp.float32), 'q_w': _uniform(ks[2], (D, D), wb), 'q_b': _uniform(ks[3], (D,), wb), 'k_w': _uniform(ks[4], (D, D), wb), 'k_b': _uniform(ks[5], (D,), wb), 'v_w': _uniform(ks[6], (D, D), wb), 'v_b': _uniform(ks[7], (D,), wb), 'o_w': _uniform(ks[8], (D, D), wb), 'o_b': _uniform(ks[9], (D,), wb)}
    _L0_ffn_in = _L0_ffn_setup()
    _d = {'L0_attn_x': _L0_attn_in['x'], 'L0_attn_in_proj_w': _L0_attn_in['in_proj_w'], 'L0_attn_in_proj_b': _L0_attn_in['in_proj_b'], 'L0_attn_out_proj_w': _L0_attn_in['out_proj_w'], 'L0_attn_out_proj_b': _L0_attn_in['out_proj_b'], 'L0_attn_ffn1_w': _L0_attn_in['ffn1_w'], 'L0_attn_ffn1_b': _L0_attn_in['ffn1_b'], 'L0_attn_ffn2_w': _L0_attn_in['ffn2_w'], 'L0_attn_ffn2_b': _L0_attn_in['ffn2_b'], 'L0_attn_ln1_w': _L0_attn_in['ln1_w'], 'L0_attn_ln1_b': _L0_attn_in['ln1_b'], 'L0_attn_ln2_w': _L0_attn_in['ln2_w'], 'L0_attn_ln2_b': _L0_attn_in['ln2_b'], 'L0_attn_final_w': _L0_attn_in['final_w'], 'L0_attn_final_b': _L0_attn_in['final_b'], 'L0_ffn_router_prob': _L0_ffn_in['router_prob'], 'L0_ffn_norm_w': _L0_ffn_in['norm_w'], 'L0_ffn_norm_b': _L0_ffn_in['norm_b'], 'L0_ffn_q_w': _L0_ffn_in['q_w'], 'L0_ffn_q_b': _L0_ffn_in['q_b'], 'L0_ffn_k_w': _L0_ffn_in['k_w'], 'L0_ffn_k_b': _L0_ffn_in['k_b'], 'L0_ffn_v_w': _L0_ffn_in['v_w'], 'L0_ffn_v_b': _L0_ffn_in['v_b'], 'L0_ffn_o_w': _L0_ffn_in['o_w'], 'L0_ffn_o_b': _L0_ffn_in['o_b']}
    _x0 = _d['L0_attn_x']
    _d['L0_attn_x'] = jax.random.normal(jax.random.fold_in(jax.random.key(seed), 1), (16, 256, 128), dtype=_x0.dtype)
    del _x0
    return _d

def reference(L0_attn_x, L0_attn_in_proj_w, L0_attn_in_proj_b, L0_attn_out_proj_w, L0_attn_out_proj_b, L0_attn_ffn1_w, L0_attn_ffn1_b, L0_attn_ffn2_w, L0_attn_ffn2_b, L0_attn_ln1_w, L0_attn_ln1_b, L0_attn_ln2_w, L0_attn_ln2_b, L0_attn_final_w, L0_attn_final_b, L0_ffn_router_prob, L0_ffn_norm_w, L0_ffn_norm_b, L0_ffn_q_w, L0_ffn_q_b, L0_ffn_k_w, L0_ffn_k_b, L0_ffn_v_w, L0_ffn_v_b, L0_ffn_o_w, L0_ffn_o_b):

    def _L0_attn_ref(x, in_proj_w, in_proj_b, out_proj_w, out_proj_b, ffn1_w, ffn1_b, ffn2_w, ffn2_b, ln1_w, ln1_b, ln2_w, ln2_b, final_w, final_b):
        import math
        import jax, jax.numpy as jnp
        import numpy as np
        L, D, H, F = (4, 128, 16, 512)
        HD = D // H
        EPS = 1e-05

        def get_alibi_slopes(num_heads):
            closest = 2 ** math.floor(math.log2(num_heads))
            base = 2 ** (-2 ** (-(math.log2(closest) - 3)))
            slopes = base ** np.arange(1, closest + 1)
            if closest != num_heads:
                extra_base = 2 ** (-2 ** (-(math.log2(2 * closest) - 3)))
                extra = extra_base ** np.arange(1, 2 * (num_heads - closest) + 1, 2)
                slopes = np.concatenate([slopes, extra])
            return jnp.asarray(slopes, dtype=jnp.float32)

        def build_mask(num_heads, T):
            pos = jnp.arange(T)
            dist = pos[None, :] - pos[:, None]
            alibi = get_alibi_slopes(num_heads)[:, None, None] * dist[None]
            causal = jnp.where(dist > 0, -jnp.inf, 0.0).astype(jnp.float32)
            return causal[None] + alibi

        def layer_norm(x, w, b):
            mu = jnp.mean(x, axis=-1, keepdims=True)
            var = jnp.mean(jnp.square(x - mu), axis=-1, keepdims=True)
            return (x - mu) * jax.lax.rsqrt(var + EPS) * w + b

        def mha(x, mask, Wi, bi, Wo, bo):
            B, T, _ = x.shape
            qkv = x @ Wi.T + bi
            q, k, v = jnp.split(qkv, 3, axis=-1)
            q = q.reshape(B, T, H, HD).transpose(0, 2, 1, 3)
            k = k.reshape(B, T, H, HD).transpose(0, 2, 1, 3)
            v = v.reshape(B, T, H, HD).transpose(0, 2, 1, 3)
            scores = jnp.einsum('bhqd,bhkd->bhqk', q, k) / math.sqrt(HD)
            scores = scores + mask[None]
            attn = jax.nn.softmax(scores, axis=-1)
            out = jnp.einsum('bhqk,bhkd->bhqd', attn, v)
            out = out.transpose(0, 2, 1, 3).reshape(B, T, D)
            return out @ Wo.T + bo
        T = x.shape[1]
        mask = build_mask(H, T)
        for i in range(L):
            xn = layer_norm(x, ln1_w[i], ln1_b[i])
            x = x + mha(xn, mask, in_proj_w[i], in_proj_b[i], out_proj_w[i], out_proj_b[i])
            xn = layer_norm(x, ln2_w[i], ln2_b[i])
            h = jax.nn.gelu(xn @ ffn1_w[i].T + ffn1_b[i], approximate=False)
            x = x + (h @ ffn2_w[i].T + ffn2_b[i])
        return layer_norm(x, final_w, final_b)

    def _L0_ffn_ref(x, router_prob, norm_w, norm_b, q_w, q_b, k_w, k_b, v_w, v_b, o_w, o_b):
        import jax, jax.numpy as jnp
        import numpy as np
        B, T, D, E, H = (4, 256, 128, 4, 8)
        EPS = 1e-05

        def _uniform(k, shape, bound):
            return jax.random.uniform(k, shape, jnp.float32, -bound, bound)

        def _layernorm(x, w, b):
            mu = jnp.mean(x, axis=-1, keepdims=True)
            var = jnp.mean(jnp.square(x - mu), axis=-1, keepdims=True)
            return (x - mu) * jax.lax.rsqrt(var + EPS) * w + b
        e_cnt = router_prob.shape[2]
        b, t, d = x.shape
        n = t // e_cnt
        h = H
        scale = d ** (-0.5)
        qs, ks_, vs = ([], [], [])
        for e in range(e_cnt):
            xe = x[:, e * n:(e + 1) * n, :]
            xn = _layernorm(xe, norm_w, norm_b)
            m = d // 2 ** e
            xm = xn[..., :m]
            qs.append(jnp.einsum('bnm,dm->bnd', xm, q_w[:, :m]) + q_b)
            ks_.append(jnp.einsum('bnm,dm->bnd', xm, k_w[:, :m]) + k_b)
            vs.append(jnp.einsum('bnm,dm->bnd', xm, v_w[:, :m]) + v_b)
        q = jnp.concatenate(qs, axis=1)
        k = jnp.concatenate(ks_, axis=1)
        v = jnp.concatenate(vs, axis=1)
        dh = d // h
        q = q.reshape(b, t, h, dh).transpose(0, 2, 1, 3)
        k = k.reshape(b, t, h, dh).transpose(0, 2, 1, 3)
        v = v.reshape(b, t, h, dh).transpose(0, 2, 1, 3)
        attn = jnp.einsum('bhqd,bhkd->bhqk', q, k) * scale
        attn = jax.nn.softmax(attn, axis=-1)
        attn_out = jnp.einsum('bhqk,bhkd->bhqd', attn, v)
        attn_out = attn_out.transpose(0, 2, 1, 3).reshape(b, t, d)
        outs = []
        for e in range(e_cnt):
            sl = slice(e * n, (e + 1) * n)
            m = d // 2 ** e
            xm = attn_out[:, sl, :m]
            out = jnp.einsum('bnm,om->bno', xm, o_w[:m, :m]) + o_b[:m]
            pad = d - m
            if pad:
                out = jnp.pad(out, ((0, 0), (0, 0), (0, pad)))
            outs.append(out + x[:, sl, :])
        return jnp.concatenate(outs, axis=1)
    x = L0_attn_x
    xn = _layernorm(x, axis=-1)
    x = x + _L0_attn_ref(xn, L0_attn_in_proj_w, L0_attn_in_proj_b, L0_attn_out_proj_w, L0_attn_out_proj_b, L0_attn_ffn1_w, L0_attn_ffn1_b, L0_attn_ffn2_w, L0_attn_ffn2_b, L0_attn_ln1_w, L0_attn_ln1_b, L0_attn_ln2_w, L0_attn_ln2_b, L0_attn_final_w, L0_attn_final_b) + _L0_ffn_ref(xn, L0_ffn_router_prob, L0_ffn_norm_w, L0_ffn_norm_b, L0_ffn_q_w, L0_ffn_q_b, L0_ffn_k_w, L0_ffn_k_b, L0_ffn_v_w, L0_ffn_v_b, L0_ffn_o_w, L0_ffn_o_b)
    return x

_drawn_inputs = setup_inputs


def setup_inputs(seed=0):
    import zlib

    import numpy as np

    out = dict(_drawn_inputs(seed))
    spreads = {'L0_attn_in_proj_b': (0.0, 2.0),
     'L0_attn_out_proj_b': (0.0, 2.0),
     'L0_attn_ffn1_b': (0.0, 2.0),
     'L0_attn_ffn2_b': (0.0, 2.0),
     'L0_attn_ln1_w': (1.0, 0.6),
     'L0_attn_ln1_b': (0.0, 2.0),
     'L0_attn_ln2_w': (1.0, 0.6),
     'L0_attn_ln2_b': (0.0, 2.0),
     'L0_attn_final_w': (1.0, 0.6),
     'L0_attn_final_b': (0.0, 0.8),
     'L0_ffn_norm_w': (1.0, 0.6),
     'L0_ffn_norm_b': (0.0, 0.8)}
    factors = {'L0_attn_in_proj_w': 18.527,
     'L0_attn_out_proj_w': 7.865,
     'L0_ffn_q_w': 8.0,
     'L0_ffn_q_b': 8.0,
     'L0_ffn_k_w': 8.0,
     'L0_ffn_k_b': 200.0,
     'L0_ffn_v_w': 8.0,
     'L0_ffn_v_b': 8.0,
     'L0_ffn_o_w': 8.0,
     'L0_ffn_o_b': 30.291,
     'L0_attn_ffn1_w': 8.0,
     'L0_attn_ffn2_w': 6.421}
    for name, (base, spread) in spreads.items():
        noise = np.random.default_rng([zlib.crc32(name.encode()), seed]).standard_normal(out[name].shape)
        drawn = base * np.exp(spread * noise) if base else spread * noise
        out[name] = jnp.asarray(drawn.astype(out[name].dtype))
    for name, factor in factors.items():
        out[name] = (out[name] * factor).astype(out[name].dtype)
    return out
```

```python
from contextlib import ExitStack

import numpy as np

import concourse.bass as bass
from concourse import mybir

F32 = mybir.dt.float32
F32R = mybir.dt.float32r
BF16 = mybir.dt.bfloat16
ALU = mybir.AluOpType
ACT = mybir.ActivationFunctionType
AX = mybir.AxisListType

P = 128
BATCH, T, D = 16, 256, 128
NT = T // P
LAYERS, FF = 4, 512
NF = FF // P
EPS = 1e-5
GROUPS = 4
CH = D // GROUPS
COPIES = 3
PARTS = ((0, 0, 1), (0, 1, 0))
ALIBI_ROW = 96
MAX_ROW = 127
MASKED = -1e30
OT_BANK = 2

A_Q, A_K, A_V, A_BV, A_BQ, A_BK, A_LNW, A_LNB, A_COLS = 0, 128, 256, 384, 512, 513, 514, 515, 516
C_O, C_BO, C_W1, C_W2, C_B2, C_LNW, C_LNB, C_B1, C_COLS = 0, 128, 256, 768, 1280, 1408, 1409, 1410, 1414
CF_COLS = 256


class Plan:

    def __init__(self, name, heads, causal, feed_forward, rounds):
        self.name, self.heads, self.causal, self.feed_forward, self.rounds = name, heads, causal, feed_forward, rounds
        self.dh = D // heads
        self.hg = heads // GROUPS
        self.scale = float(np.float32((self.dh if causal else D) ** -0.5))
        self.max_chunks = NT * self.hg // 2
        self.exp_chunks = 3 if causal else 2
        self.slot = 16 if causal else 32
        self.stack_dmas = self.hg + 1
        self.units = 2 * rounds

    def slot_steps(self, s):
        def at(names, unit):
            return [(name, unit) for name in names.split()]

        ff = self.feed_forward
        maxes = [("max", s + 1, g, ch) for g in range(GROUPS) for ch in range(self.max_chunks)]
        out = [("exp", s, 0, 0), ("exp", s, 0, 1)]
        out += at("ot", s - 1) + at("ln", s + 2) + at("ot+", s - 1) + at("xn", s + 2)
        out += at("f2 f2+", s - 2) if ff else []
        out += at("at at+", s - 1)
        after = [
            at("v v+", s + 1) + at("xt", s + 2),
            at("xt+", s + 2) + at("op", s - 1),
            at("op+", s - 1) + at("qk", s + 2),
            [("pv", s, 0)] + at("qk+", s + 2),
            [],
            at("xn2", s - 1) if ff else [],
            [("pv", s, 1)] + (at("xt2", s - 1) if ff else []),
            at("xt2+", s - 1) if ff else [],
            [],
            at("negt negt+", s + 1) + [("pv", s, 2)]]
        for k in range(2, 3 * GROUPS):
            g, ch = divmod(k, 3)
            if ch < self.exp_chunks:
                out.append(("exp", s, g, ch))
            n = self.max_chunks // 2
            out += maxes[n * (k - 2):n * (k - 1)] + after[k - 2]
        out += at("f1 f1+", s - 1) if ff else []
        return out + [("pv", s, GROUPS - 1)] + at("pv+", s) + at("stack+", s + 2)

    def steps(self, n):
        for step, off, *g in self.slot_steps(0) + self.slot_steps(1):
            u = 2 * n + off
            if not isinstance(n, int) or 0 <= u < self.units:
                yield step, u, off % 2, n + off // 2, g, off


EXPERT = Plan("F", 8, False, False, BATCH // 2)
ENCODER = Plan("L", 16, True, True, LAYERS * BATCH // 2)


class Semaphores:

    def __init__(self, sem, name):
        self.a_stats = sem(f"{name}_a_stats")
        self.a_mv = sem(f"{name}_a_mv")
        self.a_eps = sem(f"{name}_a_eps")
        self.a_rstd = sem(f"{name}_a_rstd")
        self.a_xn = sem(f"{name}_a_xn")
        self.a_xt = sem(f"{name}_a_xt")
        self.a_xnt = sem(f"{name}_a_xnt")
        self.a_mask = sem(f"{name}_a_mask")
        self.a_qk = sem(f"{name}_a_qk")
        self.a_v = sem(f"{name}_a_v")
        self.a_y = sem(f"{name}_a_y")
        self.a_hi = sem(f"{name}_a_hi")
        self.a_lo = sem(f"{name}_a_lo")
        self.a_vst = sem(f"{name}_a_vst")
        self.b_max = sem(f"{name}_b_max")
        self.b_red = sem(f"{name}_b_red")
        self.b_nt = sem(f"{name}_b_nt")
        self.b_negt = sem(f"{name}_b_negt")
        self.b_s = sem(f"{name}_b_s")
        self.b_exp = sem(f"{name}_b_exp")
        self.b_pv = sem(f"{name}_b_pv")
        self.c_ost = sem(f"{name}_c_ost")
        self.c_ot = sem(f"{name}_c_ot")
        self.c_rec = sem(f"{name}_c_rec")
        self.c_attn = sem(f"{name}_c_attn")
        self.c_at = sem(f"{name}_c_at")
        self.c_attnt = sem(f"{name}_c_attnt")
        self.c_op = sem(f"{name}_c_op")
        self.c_xb = sem(f"{name}_c_xb")
        self.c_add = sem(f"{name}_c_add")
        self.c_add2 = sem(f"{name}_c_add2")
        self.c_stats = sem(f"{name}_c_stats")
        self.c_mv = sem(f"{name}_c_mv")
        self.c_eps = sem(f"{name}_c_eps")
        self.c_rstd = sem(f"{name}_c_rstd")
        self.c_xn2 = sem(f"{name}_c_xn2")
        self.c_xt2 = sem(f"{name}_c_xt2")
        self.c_xn2t = sem(f"{name}_c_xn2t")
        self.c_f1 = sem(f"{name}_c_f1")
        self.c_gelu = sem(f"{name}_c_gelu")
        self.c_f2 = sem(f"{name}_c_f2")
        self.c_xb2 = sem(f"{name}_c_xb2")
        self.c_done = sem(f"{name}_c_done")
        self.wa = sem(f"{name}_wa")
        self.wc = sem(f"{name}_wc")
        self.wa_ok = sem(f"{name}_wa_ok")
        self.wc_ok = sem(f"{name}_wc_ok")
        self.parts = [sem(f"{name}_parts{s}") for s in range(2)]
        self.stk = [sem(f"{name}_stk{s}") for s in range(2)]
        self.nmax = [sem(f"{name}_nmax{s}") for s in range(2)]


def wait_past(eng, sem, value):
    if isinstance(value, int) and value <= 0:
        return
    eng.wait_ge(sem, value)


def settle(eng, passed):
    eng.sem_inc(passed, 1)


def rounds_of(eng, plan, body):
    body(-1)
    body(0)
    body(1)
    with eng.Fori(2, plan.rounds - 1) as n:
        body(n)
    body(plan.rounds - 1)
    body(plan.rounds)


def build(nc, x_in, wa_l, wc_l, wa_f, wc_f, fin_w, rows_q, rows_k, rows_kf, seg_in, seg_out, out):
    with ExitStack() as ctx:
        def sb(name, shape, dt=F32):
            return ctx.enter_context(nc.sbuf_tensor(name, shape, dt))

        def ps(name, shape):
            return ctx.enter_context(nc.psum_tensor(name, shape, F32))

        def sem(name):
            return ctx.enter_context(nc.semaphore(name))

        state = sb("state", [P, BATCH, NT, D])
        rest = sb("rest", [P, BATCH, NT, D])
        wa = {"F": sb("wa_f", [P, A_COLS]), "L": sb("wa_l", [P, A_COLS])}
        wc = {"F": sb("wc_f", [P, CF_COLS]), "L": sb("wc_l", [P, C_COLS])}
        fin = sb("fin", [P, 2, D])
        seg_rows = sb("seg_rows", [P, T])
        seg_cols = sb("seg_cols", [P, NT, D])
        qbd = {"L": sb("qbd_l", [P, 2, ENCODER.heads, T], F32R), "F": sb("qbd_f", [P, 2, EXPERT.heads, T], F32R)}
        kst = {"L": sb("kst_l", [P, 2, GROUPS, T], F32R), "F": sb("kst_f", [P, 2, GROUPS, T], F32R)}
        probs = sb("probs", [P, GROUPS, 3, 512])
        vst = {"L": sb("vst_l", [P, 2, NT, 2, 8, 32]), "F": sb("vst_f", [P, 2, NT, 1, 8, 32])}
        stats = sb("stats", [P, 2, 2, NT, 6])
        mv = sb("mv", [P, 2, 2, NT, 2])
        veps = sb("veps", [P, 2, 2, NT])
        rstd = sb("rstd", [P, 2, 2, NT])
        stats_all = sb("stats_all", [P, BATCH * NT, 6])
        mv_all = sb("mv_all", [P, BATCH * NT, 2])
        veps_all = sb("veps_all", [P, BATCH * NT])
        rstd_all = sb("rstd_all", [P, BATCH * NT])
        half = sb("half", [P, BATCH * NT])
        xn = sb("xn", [P, 2, 2, NT, D])
        xnt = sb("xnt", [P, 2, 2, T])
        y = sb("y", [P, 2, 2 * T])
        hi = sb("hi", [P, 2, 2 * T], F32R)
        lo = sb("lo", [P, 2, 2 * T], F32R)
        negm = sb("negm", [P, 2, NT, 16])
        negt = sb("negt", [16, 2, NT, P], F32R)
        ost = sb("ost", [P, 2, 2, T])
        rec = sb("rec", [P, 2, 32])
        attn = sb("attn", [P, 2, NT, D])
        attnt = sb("attnt", [P, 2, T])
        xb = sb("xb", [P, 2, NT, D])
        xb2 = sb("xb2", [P, 2, NT, D])
        tmp = sb("tmp", [P, 2, NT, D])
        hid = sb("hid", [P, 2, NF, T])
        fo = sb("fo", [P, 2, NT, D])
        ident = sb("ident", [P, P])
        identb = sb("identb", [P, P], BF16)
        maskf = sb("maskf", [P, 2, P])
        maskb = sb("maskb", [P, 2, P], BF16)
        masktf = sb("masktf", [P, 4, P])
        masktb = sb("masktb", [P, 4, P], BF16)

        split = {p.name: nc.dram_tensor(f"split_{p.name}", [2, 2, p.hg, COPIES, p.dh, GROUPS * T], F32,
                                        kind="Internal").ap() for p in (EXPERT, ENCODER)}

        dense = [ps("dense0", [P, 512]), ps("dense1", [P, 512])]
        mxp = ps("mxp", [P, 3, 512])
        exp_ps = ps("exp_ps", [P, 2, 512])
        pvp = ps("pvp", [P, 512])

        s_x = sem("s_x")
        s_w = sem("s_w")
        s_init = sem("s_init")
        s_initv = sem("s_initv")
        s_rows = sem("s_rows")
        s_stats = sem("s_stats")
        s_mv = sem("s_mv")
        s_eps = sem("s_eps")
        s_rstd = sem("s_rstd")
        s_norm = sem("s_norm")
        s_final = sem("s_final")
        s_store = [sem(f"s_store{s}") for s in range(2)]
        passed_dve, passed_pool, passed_sp = sem("passed_dve"), sem("passed_pool"), sem("passed_sp")
        S = {p.name: Semaphores(sem, p.name) for p in (EXPERT, ENCODER)}

        rq = hid[0:32, :, :, :].rearrange("p a b c -> p (a b c)")
        rk = y[0:32, :, :].rearrange("p a b -> p (a b)")
        rkf = ost[0:32, :, :, :].rearrange("p a b c -> p (a b c)")

        block = ctx.enter_context(nc.Block())

        @block.sync
        def _(sp):
            xv = x_in.rearrange("b (t p) d -> p b t d", p=P)
            for k in range(4):
                sp.dma_start(rest[:, 4 * k:4 * k + 4, :, :], xv[:, 4 * k:4 * k + 4, :, :]).then_inc(s_x, 16)
            sp.dma_start(rk, rows_k).then_inc(s_rows, 16)
            sp.dma_start(rkf, rows_kf).then_inc(s_rows, 16)
            sp.dma_start(rq, rows_q[:, 0:2048]).then_inc(s_rows, 16)
            for dst, src in ((wa["F"], wa_f), (wc["F"], wc_f), (fin, fin_w), (seg_rows, seg_in), (seg_cols, seg_out)):
                sp.dma_start(dst[:], src).then_inc(s_w, 16)
            sp.wait_ge(s_initv, 3)
            sp.dma_start(rq, rows_q[:, 2048:4096]).then_inc(s_rows, 16)

            def keep_parts(plan, q, u, r, s):
                wait_past(sp, q.stk[s], 16 * plan.stack_dmas * r)
                settle(sp, passed_sp)
                for part, ready, source in ((0, q.a_hi, hi), (1, q.a_lo, lo)):
                    sp.wait_ge(ready, u + 1)
                    for qk in range(2):
                        for copy in range(COPIES):
                            if PARTS[qk][copy] == part:
                                dst = split[plan.name][s, qk, :, copy].rearrange("i d (g t) -> i (d g) t", t=T)
                                sp.dma_start(dst, source[:, s, qk * T:(qk + 1) * T].bitcast(F32)).then_inc(q.parts[s], 16)

            def stack_queries_and_keys(plan, q, u, r, s):
                sc = split[plan.name][s]
                sp.wait_ge(q.parts[s], 16 * 2 * COPIES * (r + 1))
                settle(sp, passed_sp)
                wait_past(sp, q.b_s, plan.exp_chunks * GROUPS * (u - 1))
                settle(sp, passed_sp)
                rows = COPIES * plan.dh
                sp.dma_start(kst[plan.name][0:plan.hg * rows, s, :, :].bitcast(F32),
                             sc[1].rearrange("i c d (g t) -> (i c d) g t", t=T)).then_inc(q.stk[s], 16)
                qd = qbd[plan.name][:, s].bitcast(F32).rearrange("p (g i) t -> p g i t", g=GROUPS)
                for i in range(plan.hg):
                    sp.dma_start(qd[i * rows:(i + 1) * rows, :, i, :],
                                 sc[0, i].rearrange("c d (g t) -> (c d) g t", t=T)).then_inc(q.stk[s], 16)

            def share(plan, q, step, u, s, r):
                if step == "qk+":
                    keep_parts(plan, q, u, r, s)
                elif step == "stack+":
                    stack_queries_and_keys(plan, q, u, r, s)
                elif step == "negt+":
                    sp.wait_ge(q.b_negt, u + 1)
                    sp.dma_start(qbd[plan.name][MAX_ROW:MAX_ROW + 1, s, :, :].bitcast(F32),
                                 negt[0:plan.heads, s, :, :].bitcast(F32)).then_inc(q.nmax[s], 16)

            def expert_round(n):
                for step, u, s, r, *_ in EXPERT.steps(n):
                    share(EXPERT, S["F"], step, u, s, r)

            rounds_of(sp, EXPERT, expert_round)

            q, per = S["L"], BATCH // 2
            sp.dma_start(wa["L"][:], wa_l[0]).then_inc(q.wa, 16)
            sp.wait_ge(S["F"].c_done, BATCH)
            sp.wait_ge(q.wa, 16)

            def load_a(layer):
                sp.wait_ge(q.a_vst, BATCH * layer)
                settle(sp, passed_sp)
                sp.dma_start(wa["L"][:], wa_l[layer]).then_inc(q.wa, 16)
                sp.wait_ge(q.wa, 16 * (layer + 1))
                settle(sp, passed_sp)

            def load_c(layer):
                sp.wait_ge(q.c_done, BATCH * (layer + 1))
                settle(sp, passed_sp)
                sp.dma_start(wc["L"][:], wc_l[layer]).then_inc(q.wc, 16)
                sp.wait_ge(q.wc, 16 * (layer + 1))
                settle(sp, passed_sp)

            def encoder_round(n, first_of=None, last_of=None):
                for step, u, s, r, *_ in ENCODER.steps(n):
                    share(ENCODER, q, step, u, s, r)
                    if step == "xt" and s == 0:
                        if last_of is not None:
                            load_a(last_of + 1)
                        sp.sem_inc(q.wa_ok, 1)
                    if step == "op":
                        if first_of is not None and s == 0:
                            load_c(first_of)
                        sp.sem_inc(q.wc_ok, 1)

            def layer_rounds(layer, last=False):
                with sp.Fori(1, per - 1) as j:
                    encoder_round(per * layer + j)
                encoder_round(per * layer + per - 1, last_of=None if last else layer)

            encoder_round(-1)
            encoder_round(0, first_of=0)
            encoder_round(1)
            with sp.Fori(2, per - 1) as j:
                encoder_round(j)
            encoder_round(per - 1, last_of=0)
            with sp.Fori(1, LAYERS - 1) as layer:
                encoder_round(per * layer, first_of=layer)
                layer_rounds(layer)
            encoder_round(per * (LAYERS - 1), first_of=LAYERS - 1)
            layer_rounds(LAYERS - 1, last=True)
            encoder_round(per * LAYERS)

            ov = out.rearrange("b (t p) d -> b p t d", p=P)
            with sp.Fori(0, BATCH // 2) as m:
                for s in range(2):
                    sp.wait_ge(s_final, 2 * m + s + 1)
                    sp.dma_start(ov[2 * m + s], fo[:, s, :, :]).then_inc(s_store[s], 16)
            for s in range(2):
                sp.wait_ge(s_store[s], 16 * BATCH // 2)

        @block.gpsimd
        def _(pool):
            pool.memset(ident[:], 0.0).then_inc(s_init, 1)
            pool.memset(maskf[:], 0.0).then_inc(s_init, 1)
            pool.memset(half[:], -0.5).then_inc(s_init, 1)
            pool.memset(masktf[:], 0.0).then_inc(s_init, 1)
            pool.wait_ge(s_init, 4)
            pool.affine_select(out=ident[:], in_=ident[:], compare_op=ALU.not_equal, fill=1.0, base=0,
                               pattern=[[-1, P]], channel_multiplier=1).then_inc(s_init, 1)
            pool.affine_select(out=maskf[:], in_=maskf[:], compare_op=ALU.is_ge, fill=MASKED, base=0,
                               pattern=[[0, 2], [-1, P]], channel_multiplier=1).then_inc(s_init, 1)
            pool.affine_select(out=masktf[:], in_=masktf[:], compare_op=ALU.is_ge, fill=MASKED, base=0,
                               pattern=[[0, 4], [1, P]], channel_multiplier=-1).then_inc(s_init, 1)
            pool.wait_ge(s_init, 7)
            pool.tensor_copy(identb[:], ident[:]).then_inc(s_init, 1)
            pool.tensor_copy(maskb[:], maskf[:]).then_inc(s_init, 1)
            pool.tensor_copy(masktb[:], masktf[:]).then_inc(s_init, 1)

            def inverse_deviation_of_all(k):
                pool.wait_ge(s_mv, k)
                pool.tensor_scalar(veps_all[:], mv_all[:, :, 1], EPS, None, ALU.add).then_inc(s_eps, 1)
                pool.wait_ge(s_eps, k)
                pool.tensor_tensor(rstd_all[:], veps_all[:], half[:], ALU.pow).then_inc(s_rstd, 1)

            def inverse_deviation(q, stage, u, s):
                k = "AC".index(stage)
                ready, eps, done = (q.a_mv, q.a_eps, q.a_rstd) if stage == "A" else (q.c_mv, q.c_eps, q.c_rstd)
                pool.wait_ge(ready, u + 1)
                settle(pool, passed_pool)
                pool.tensor_scalar(veps[:, k, s, :], mv[:, k, s, :, 1], EPS, None, ALU.add).then_inc(eps, 1)
                pool.wait_ge(eps, u + 1)
                pool.tensor_tensor(rstd[:, k, s, :], veps[:, k, s, :], half[:, 0:NT], ALU.pow).then_inc(done, 1)

            def steps(plan, n):
                q = S[plan.name]
                for step, u, s, r, g, _ in plan.steps(n):
                    if step == "ln":
                        inverse_deviation(q, "A", u, s)
                    elif step == "qk+":
                        pool.wait_ge(q.a_hi, u + 1)
                        wait_past(pool, q.parts[s], 16 * 2 * COPIES * r)
                        pool.tensor_tensor(lo[:, s, :], y[:, s, :], hi[:, s, :].bitcast(F32), ALU.subtract)\
                            .then_inc(q.a_lo, 1)
                    elif step == "op":
                        if plan.causal:
                            bt = u % BATCH
                            pool.wait_ge(q.c_done, u + 1)
                            pool.wait_ge(q.wc_ok, u + 1)
                            wait_past(pool, q.c_add, u - 1)
                            settle(pool, passed_pool)
                            for t in range(NT):
                                last = pool.tensor_tensor(xb[:, s, t, :], state[:, bt, t, :], wc["L"][:, C_BO:C_BO + D], ALU.add)
                            last.then_inc(q.c_xb, 1)
                        else:
                            pool.wait_ge(s_norm, u + 1)
                            wait_past(pool, q.c_done, u - 1)
                            settle(pool, passed_pool)
                            pool.tensor_tensor(xb[:, s, :, :], state[:, u, :, :], rest[:, u, :, :], ALU.add)\
                                .then_inc(q.c_xb, 1)
                    elif step == "op+" and plan.feed_forward:
                        inverse_deviation(q, "C", u, s)
                        wait_past(pool, q.c_done, BATCH + u - 1)
                        settle(pool, passed_pool)
                        for t in range(NT):
                            last = pool.tensor_tensor(xb2[:, s, t, :], state[:, u % BATCH, t, :], wc["L"][:, C_B2:C_B2 + D], ALU.add)
                        last.then_inc(q.c_xb2, 1)

            inverse_deviation_of_all(1)
            pool.wait_ge(s_w, 16 * 5)
            rounds_of(pool, EXPERT, lambda n: steps(EXPERT, n))
            pool.wait_ge(S["F"].c_done, BATCH)
            rounds_of(pool, ENCODER, lambda n: steps(ENCODER, n))
            inverse_deviation_of_all(2)

        @block.vector
        def _(dve):
            init = [0]

            def initial(ins):
                init[0] += 1
                ins.then_inc(s_initv, 1)

            initial(dve.memset(qbd["L"][:].bitcast(F32), 0.0))
            initial(dve.memset(kst["L"][:].bitcast(F32), 0.0))
            dve.wait_ge(s_rows, 16 * 3)
            dve.wait_ge(s_initv, 2)
            q_rows = qbd["L"][ALIBI_ROW:P, :, :, :].rearrange("p s h t -> p s (h t)")
            initial(dve.tensor_copy(q_rows[:, 0, 0:2048], rq))
            dve.wait_ge(s_initv, 3)

            def stats_of_all(source, k):
                with dve.Fori(0, BATCH) as b:
                    for t in range(NT):
                        last = dve.bn_stats(stats_all[:, b * NT + t, :], source[:, b, t, :])
                    last.then_inc(s_stats, 1)
                dve.wait_ge(s_stats, BATCH * k)
                for r in range(BATCH * NT):
                    last = dve.bn_aggr(mv_all[:, r, :], stats_all[:, r, :])
                last.then_inc(s_mv, 1)

            dve.wait_ge(s_x, 64)
            stats_of_all(rest, 1)
            initial(dve.memset(qbd["F"][:].bitcast(F32), 0.0))
            initial(dve.memset(kst["F"][:].bitcast(F32), 0.0))
            initial(dve.memset(vst["F"][:], 0.0))
            initial(dve.memset(vst["L"][:], 0.0))
            dve.wait_ge(s_initv, init[0])
            initial(dve.memset(vst["F"][:, :, :, :, :, 16:17], 1.0))
            initial(dve.memset(vst["L"][:, :, :, 0, :, 8:9], 1.0))
            initial(dve.memset(vst["L"][:, :, :, 1, :, 24:25], 1.0))
            initial(dve.tensor_copy(q_rows[:, 1, 0:2048], q_rows[:, 0, 0:2048].bitcast(F32)))
            dve.wait_ge(s_rows, 16 * 4)
            for s in range(2):
                initial(dve.tensor_copy(q_rows[:, s, 2048:4096], rq))
                initial(dve.tensor_copy(kst["L"][ALIBI_ROW:P, s, :, :].rearrange("p g t -> p (g t)"), rk))
                initial(dve.tensor_copy(kst["F"][ALIBI_ROW:P, s, :, :].rearrange("p g t -> p (g t)"), rkf))
            dve.wait_ge(s_initv, init[0])
            dve.wait_ge(s_rstd, 1)
            with dve.Fori(0, BATCH) as b:
                for t in range(NT):
                    r = b * NT + t
                    last = dve.tensor_scalar(state[:, b, t, :], rest[:, b, t, :], mv_all[:, r, 0:1],
                                             rstd_all[:, bass.ds(r, 1)], ALU.subtract, ALU.mult)
                last.then_inc(s_norm, 1)
            dve.wait_ge(s_w, 16 * 5)

            def statistics(q, stage, u, s, source):
                k = "AC".index(stage)
                done, ready = (q.a_stats, q.a_mv) if stage == "A" else (q.c_stats, q.c_mv)
                settle(dve, passed_dve)
                for t in range(NT):
                    last = dve.bn_stats(stats[:, k, s, t, :], source[:, t, :])
                last.then_inc(done, 1)
                dve.wait_ge(done, u + 1)
                settle(dve, passed_dve)
                for t in range(NT):
                    last = dve.bn_aggr(mv[:, k, s, t, :], stats[:, k, s, t, :])
                last.then_inc(ready, 1)

            def normalise(q, stage, u, s, source):
                k = "AC".index(stage)
                rstd_ready, used, done = (q.a_rstd, q.a_xt, q.a_xn) if stage == "A" else (q.c_rstd, q.c_xt2, q.c_xn2)
                dve.wait_ge(rstd_ready, u + 1)
                wait_past(dve, used, u - 1)
                for t in range(NT):
                    last = dve.tensor_scalar(xn[:, k, s, t, :], source[:, t, :], mv[:, k, s, t, 0:1],
                                             rstd[:, k, s, t:t + 1], ALU.subtract, ALU.mult)
                last.then_inc(done, 1)

            def high_parts(q, u, r, s):
                dve.wait_ge(q.a_y, 2 * (u + 1))
                wait_past(dve, q.parts[s], 16 * 2 * COPIES * r)
                dve.tensor_copy(hi[:, s, :], y[:, s, :]).then_inc(q.a_hi, 1)

            def place_values(plan, q, u, s):
                dve.wait_ge(q.a_v, u + 1)
                wait_past(dve, q.b_pv, GROUPS * (u - 1))
                bias = wa[plan.name][:, A_BV:A_BV + D]
                halves = 2 if plan.causal else 1
                for h in range(halves):
                    width = D // halves
                    for t in range(NT):
                        i0 = dense[0][:, t * D + h * width:t * D + (h + 1) * width].rearrange("p (h d) -> p h d", d=plan.dh)
                        i1 = bias[:, h * width:(h + 1) * width].rearrange("p (h d) -> p h d", d=plan.dh)
                        o = vst[plan.name][:, s, t, h, :, plan.slot * h:plan.slot * h + plan.dh]
                        last = dve.tensor_tensor(o, i0, i1, ALU.add)
                last.then_inc(q.a_vst, 1)

            def maxima(plan, q, u, s, g, ch):
                c = plan.max_chunks * (GROUPS * u + g) + ch
                qt, pair = ch % NT, ch // NT
                dve.wait_ge(q.b_max, c + 1)
                if g == 0 and ch == 0:
                    wait_past(dve, q.b_nt, u - 1)
                keys = P if plan.causal and qt == 0 else T
                h0 = plan.hg * g + 2 * pair
                dve.tensor_reduce(negm[:, s, qt, h0:h0 + 2],
                                  mxp[:, (plan.max_chunks * g + ch) % 3, :].rearrange("p (h t) -> p h t", h=2)[:, :, 0:keys],
                                  AX.X, ALU.max, negate=True).then_inc(q.b_red, 1)

            def divide_by_sums(plan, q, u, s):
                slots = P // plan.slot * 4
                v = mxp[:, OT_BANK, :].rearrange("p (a c) -> p a c", c=plan.slot)
                dve.wait_ge(q.c_ot, u + 1)
                dve.reciprocal(rec[:, s, 0:slots], v[:, :, plan.dh]).then_inc(q.c_rec, 1)
                dve.wait_ge(q.c_rec, u + 1)
                wait_past(dve, q.c_at, u - 1)
                r = rec[:, s, 0:slots].unsqueeze(2).to_broadcast([P, slots, plan.dh])
                o = attn[:, s, :, :].rearrange("p t (a d) -> p (t a) d", d=plan.dh)
                dve.tensor_tensor(o, v[:, :, 0:plan.dh], r, ALU.mult).then_inc(q.c_attn, 1)

            def steps(plan, n):
                q = S[plan.name]
                for step, u, s, r, g, _ in plan.steps(n):
                    bt = u % BATCH if plan.causal else u
                    if step == "ln":
                        if plan.causal:
                            dve.wait_ge(q.c_done, u + 1)
                        else:
                            dve.wait_ge(s_norm, u + 1)
                        statistics(q, "A", u, s, state[:, bt])
                    elif step == "xn":
                        normalise(q, "A", u, s, state[:, bt])
                    elif step == "xt+" and not plan.causal:
                        dve.wait_ge(q.a_xnt, u + 1)
                        dve.tensor_tensor(xnt[:, 0, s, :], xnt[:, 0, s, :], seg_rows[:], ALU.mult).then_inc(q.a_mask, 1)
                    elif step == "qk+":
                        high_parts(q, u, r, s)
                    elif step == "v+":
                        place_values(plan, q, u, s)
                    elif step == "max":
                        maxima(plan, q, u, s, *g)
                    elif step == "negt+":
                        dve.wait_ge(q.b_nt, u + 1)
                        wait_past(dve, q.nmax[s], 16 * r)
                        dve.tensor_copy(negt[0:plan.heads, s, :, :],
                                        dense[1][0:plan.heads, 0:T].rearrange("p (t c) -> p t c", t=NT))\
                           .then_inc(q.b_negt, 1)
                    elif step == "pv+":
                        dve.wait_ge(q.b_pv, GROUPS * (u + 1))
                        wait_past(dve, q.c_ot, u - 1)
                        dve.tensor_copy(ost[:, s, :, :].rearrange("p r t -> p (r t)"), pvp[:, :]).then_inc(q.c_ost, 1)
                    elif step == "ot+":
                        divide_by_sums(plan, q, u, s)
                    elif step == "at+" and not plan.causal:
                        dve.wait_ge(q.c_at, u + 1)
                        wait_past(dve, q.c_op, u - 1)
                        dve.tensor_tensor(attnt[:, s, :], dense[1][:, 0:T], seg_rows[:], ALU.mult).then_inc(q.c_attnt, 1)
                    elif step == "op+":
                        projected = dense[0][:, 0:T].rearrange("p (t d) -> p t d", t=NT)
                        dve.wait_ge(q.c_op, u + 1)
                        if plan.feed_forward:
                            dve.wait_ge(q.c_xb, u + 1)
                            dve.tensor_tensor(state[:, bt, :, :], projected, xb[:, s, :, :], ALU.add).then_inc(q.c_add, 1)
                            dve.wait_ge(q.c_add, u + 1)
                            statistics(q, "C", u, s, state[:, bt])
                        else:
                            bias = wc["F"][:, C_BO:C_BO + D].unsqueeze(1).to_broadcast([P, NT, D])
                            dve.tensor_tensor(tmp[:, s, :, :], projected, bias, ALU.add).then_inc(q.c_add, 1)
                            dve.wait_ge(q.c_add, u + 1)
                            dve.tensor_tensor(tmp[:, s, :, :], tmp[:, s, :, :], seg_cols[:], ALU.mult).then_inc(q.c_add2, 1)
                            dve.wait_ge(q.c_add2, u + 1)
                            dve.wait_ge(q.c_xb, u + 1)
                            dve.tensor_tensor(rest[:, bt, :, :], tmp[:, s, :, :], xb[:, s, :, :], ALU.add).then_inc(q.c_done, 1)
                    elif step == "xn2":
                        normalise(q, "C", u, s, state[:, bt])
                    elif step == "f2+":
                        dve.wait_ge(q.c_f2, u + 1)
                        dve.wait_ge(q.c_xb2, u + 1)
                        dve.tensor_tensor(state[:, bt, :, :], dense[0][:, 0:T].rearrange("p (t d) -> p t d", t=NT),
                                          xb2[:, s, :, :], ALU.add).then_inc(q.c_done, 1)

            rounds_of(dve, EXPERT, lambda n: steps(EXPERT, n))
            dve.wait_ge(S["F"].c_done, BATCH)
            dve.memset(rec[:, 0, 0:1], 0.0).then_inc(S["L"].c_done, BATCH)
            rounds_of(dve, ENCODER, lambda n: steps(ENCODER, n))

            dve.wait_ge(S["L"].c_done, BATCH * (LAYERS + 1))
            stats_of_all(state, 2)
            dve.wait_ge(s_rstd, 2)
            weight = fin[:, 0, :].unsqueeze(1).to_broadcast([P, NT, D])
            bias = fin[:, 1, :].unsqueeze(1).to_broadcast([P, NT, D])

            def finish(m, s):
                b = 2 * m + s
                for t in range(NT):
                    r = b * NT + t
                    last = dve.tensor_scalar(tmp[:, s, t, :], state[:, b, t, :], mv_all[:, r, 0:1],
                                             rstd_all[:, bass.ds(r, 1)], ALU.subtract, ALU.mult)
                last.then_inc(s_norm, 1)
                dve.wait_ge(s_norm, BATCH + 3 * b + 1)
                dve.tensor_tensor(tmp[:, s, :, :], tmp[:, s, :, :], weight, ALU.mult).then_inc(s_norm, 1)
                dve.tensor_tensor(rest[:, b, :, :], rest[:, b, :, :], bias, ALU.add).then_inc(s_norm, 1)
                dve.wait_ge(s_norm, BATCH + 3 * b + 3)
                wait_past(dve, s_store[s], 16 * m)
                dve.tensor_tensor(fo[:, s, :, :], tmp[:, s, :, :], rest[:, b, :, :], ALU.add).then_inc(s_final, 1)

            finish(0, 0)
            finish(0, 1)
            with dve.Fori(1, BATCH // 2) as m:
                for s in range(2):
                    finish(m, s)

        @block.scalar
        def _(act):
            act.wait_ge(s_w, 16 * 5)

            def steps(plan, n):
                q = S[plan.name]
                for step, u, s, r, g, _ in plan.steps(n):
                    if step == "xt+":
                        w = wa[plan.name]
                        act.wait_ge(q.a_xt, u + 1)
                        wait_past(act, q.a_v, u - 1)
                        act.activation(xnt[:, 0, s, :], dense[1][:, 0:T], ACT.Identity, bias=w[:, A_LNB:A_LNB + 1],
                                       scale=w[:, A_LNW:A_LNW + 1]).then_inc(q.a_xnt, 1)
                    elif step == "qk+":
                        w = wa[plan.name]
                        act.wait_ge(q.a_qk, u + 1)
                        wait_past(act, q.a_lo, u - 1)
                        for k, col in enumerate((A_BQ, A_BK)):
                            act.activation(y[:, s, k * T:(k + 1) * T], dense[1][:, k * T:(k + 1) * T], ACT.Identity,
                                           bias=w[:, col:col + 1]).then_inc(q.a_y, 1)
                    elif step == "exp":
                        G, ch = GROUPS * u + g[0], g[1]
                        if ch == 0:
                            wait_past(act, q.b_pv, G - GROUPS + 1)
                        act.wait_ge(q.b_s, plan.exp_chunks * G + ch + 1)
                        act.activation(probs[:, g[0], ch, :], exp_ps[:, (plan.exp_chunks * g[0] + ch) % 2, :], ACT.Exp,
                                       scale=plan.scale).then_inc(q.b_exp, 1)
                    elif step == "at+" and plan.causal:
                        act.wait_ge(q.c_at, u + 1)
                        wait_past(act, q.c_op, u - 1)
                        act.activation(attnt[:, s, :], dense[1][:, 0:T], ACT.Copy).then_inc(q.c_attnt, 1)
                    elif step == "xt2+":
                        w = wc["L"]
                        act.wait_ge(q.c_xt2, u + 1)
                        wait_past(act, q.c_f1, 2 * (u - 1))
                        act.activation(xnt[:, 1, s, :], dense[0][:, 0:T], ACT.Identity, bias=w[:, C_LNB:C_LNB + 1],
                                       scale=w[:, C_LNW:C_LNW + 1]).then_inc(q.c_xn2t, 1)
                    elif step == "f1+":
                        wait_past(act, q.c_f2, u - 1)
                        for f in range(NF):
                            if f % 2 == 0:
                                act.wait_ge(q.c_f1, 2 * u + f // 2 + 1)
                            act.activation(hid[:, s, f, :], dense[f // 2][:, (f % 2) * T:(f % 2 + 1) * T], ACT.Gelu,
                                           bias=wc["L"][:, C_B1 + f:C_B1 + f + 1]).then_inc(q.c_gelu, 1)

            rounds_of(act, EXPERT, lambda n: steps(EXPERT, n))
            act.wait_ge(S["F"].c_done, BATCH)
            rounds_of(act, ENCODER, lambda n: steps(ENCODER, n))

        @block.tensor
        def _(pe):
            def transposes(out_bank, sources, done):
                for k, src in enumerate(sources):
                    width = src.shape[0]
                    last = pe.transpose(out_bank[0:src.shape[1], k * width:(k + 1) * width], src, ident[:, :])
                last.then_inc(done, 1)

            def steps(plan, n, read):
                q = S[plan.name]

                def dense_job(bank, sem, count, unit_offset):
                    if read[bank] is not None:
                        before, per_round, constant = read[bank]
                        pe.wait_ge(before, per_round * n + constant)
                    read[bank] = (sem, 2 * count, count * (unit_offset + 1))

                for step, u, s, r, g, off in plan.steps(n):
                    if step == "xt":
                        if plan.causal:
                            pe.wait_ge(q.wa_ok, n + 2)
                        pe.wait_ge(q.a_xn, u + 1)
                        dense_job(1, q.a_xnt, 1, off)
                        transposes(dense[1], [xn[:, 0, s, t, :] for t in range(NT)], q.a_xt)
                    elif step == "qk":
                        w = wa[plan.name]
                        pe.wait_ge(q.a_xnt if plan.causal else q.a_mask, u + 1)
                        dense_job(1, q.a_y, 2, off)
                        for k, col in enumerate((A_Q, A_K)):
                            last = pe.matmul(dense[1][:, k * T:(k + 1) * T], w[:, col:col + D], xnt[:, 0, s, :],
                                             start=True, stop=True)
                        last.then_inc(q.a_qk, 1)
                    elif step == "v":
                        w = wa[plan.name]
                        dense_job(0, q.a_vst, 1, off)
                        for t in range(NT):
                            last = pe.matmul(dense[0][:, t * D:(t + 1) * D], xnt[:, 0, s, t * P:(t + 1) * P],
                                             w[:, A_V:A_V + D], start=True, stop=True)
                        last.then_inc(q.a_v, 1)
                    elif step == "max":
                        ch = g[1]
                        if g == [0, 0]:
                            pe.wait_ge(q.stk[s], 16 * plan.stack_dmas * (r + 1))
                        k_unit = plan.max_chunks * g[0] + ch
                        bank = k_unit % 3
                        if k_unit >= 3:
                            pe.wait_ge(q.b_red, plan.max_chunks * GROUPS * u + k_unit - 2)
                        if k_unit == OT_BANK:
                            wait_past(pe, q.c_attn, u - 1)
                        qt, pair = ch % NT, ch // NT
                        for k in range(2):
                            h = plan.hg * g[0] + 2 * pair + k
                            last = pe.matmul(mxp[:, bank, k * T:(k + 1) * T],
                                             qbd[plan.name][0:MAX_ROW, s, h, qt * P:(qt + 1) * P],
                                             kst[plan.name][0:MAX_ROW, s, g[0], :],
                                             start=(k == 0), stop=True, skip_group_check=True)
                        if plan.causal:
                            o = mxp[:, bank, :].rearrange("p (h t) -> p h t", h=2)[:, :, qt * P:(qt + 1) * P]
                            last = pe.matmul(o, identb[:, :], maskb[:, :, :], start=False, stop=True,
                                             skip_group_check=True)
                        last.then_inc(q.b_max, 1)
                    elif step == "negt":
                        pe.wait_ge(q.b_red, GROUPS * plan.max_chunks * (u + 1))
                        dense_job(1, q.b_negt, 1, off)
                        transposes(dense[1], [negm[:, s, t, 0:plan.heads] for t in range(NT)], q.b_nt)
                    elif step == "exp":
                        ch, h0 = g[1], plan.hg * g[0]
                        if g == [0, 0]:
                            pe.wait_ge(q.nmax[s], 16 * (r + 1))
                        bank = (plan.exp_chunks * g[0] + ch) % 2
                        wait_past(pe, q.b_exp, plan.exp_chunks * (GROUPS * u + g[0]) + ch - 1)
                        if not plan.causal:
                            kt, rhs = ch, qbd["F"][:, s, h0:h0 + 2, :]
                        elif ch < 2:
                            kt, rhs = 0, qbd["L"][:, s, h0 + 2 * ch:h0 + 2 * ch + 2, :]
                        else:
                            kt, rhs = 1, qbd["L"][:, s, h0:h0 + 4, P:T]
                        last = pe.matmul(exp_ps[:, bank, :], kst[plan.name][:, s, g[0], kt * P:(kt + 1) * P], rhs,
                                         start=True, stop=True, skip_group_check=True)
                        if plan.causal:
                            heads = 4 if kt else 2
                            o = exp_ps[:, bank, :].rearrange("p (h t) -> p h t", h=heads)[:, :, 0:P]
                            last = pe.matmul(o, identb[:, :], masktb[:, 0:heads, :], start=False, stop=True,
                                             skip_group_check=True)
                        last.then_inc(q.b_s, 1)
                    elif step == "pv":
                        G = GROUPS * u + g[0]
                        if g[0] == 0:
                            pe.wait_ge(q.a_vst, u + 1)
                            wait_past(pe, q.c_ost, u)
                        pe.wait_ge(q.b_exp, plan.exp_chunks * (G + 1))
                        region, half_ = g[0] // 2, g[0] % 2
                        for kt in range(NT):
                            for i in range(plan.hg):
                                if plan.causal:
                                    col, lead = i, half_ == 0 and kt == 0
                                    q0 = P * kt
                                    src = (probs[:, g[0], i // 2, (i % 2) * T:(i % 2 + 1) * T] if kt == 0 else
                                           probs[:, g[0], 2, i * P:(i + 1) * P])
                                    v = vst["L"][:, s, kt, half_, 4 * region + i, :]
                                    fin_ = half_ == 1 and kt == NT - 1
                                else:
                                    col, lead, q0 = 2 * half_ + i, kt == 0, 0
                                    src = probs[:, g[0], kt, i * T:(i + 1) * T]
                                    v = vst["F"][:, s, kt, 0, 4 * region + col, :]
                                    fin_ = kt == NT - 1
                                last = pe.matmul(pvp[32 * col:32 * col + 32, region * T + q0:(region + 1) * T], v, src,
                                                 start=lead, stop=fin_, skip_group_check=True,
                                                 tile_position=(0, 32 * col))
                        last.then_inc(q.b_pv, 1)
                    elif step == "ot":
                        pe.wait_ge(q.c_ost, u + 1)
                        transposes(mxp[:, OT_BANK, :], [ost[:, s, r, t * P:(t + 1) * P] for t in range(NT) for r in range(2)], q.c_ot)
                    elif step == "at":
                        pe.wait_ge(q.c_attn, u + 1)
                        dense_job(1, q.c_attnt, 1, off)
                        transposes(dense[1], [attn[:, s, t, :] for t in range(NT)], q.c_at)
                    elif step == "op":
                        if plan.causal:
                            pe.wait_ge(q.wc_ok, u + 1)
                        pe.wait_ge(q.c_attnt, u + 1)
                        dense_job(0, q.c_add, 1, off)
                        for t in range(NT):
                            last = pe.matmul(dense[0][:, t * D:(t + 1) * D], attnt[:, s, t * P:(t + 1) * P],
                                             wc[plan.name][:, C_O:C_O + D], start=True, stop=True)
                        last.then_inc(q.c_op, 1)
                    elif step == "xt2":
                        pe.wait_ge(q.c_xn2, u + 1)
                        dense_job(0, q.c_xn2t, 1, off)
                        transposes(dense[0], [xn[:, 1, s, t, :] for t in range(NT)], q.c_xt2)
                    elif step == "f1":
                        pe.wait_ge(q.c_xn2t, u + 1)
                        for k in range(2):
                            dense_job(k, q.c_gelu, NF, off)
                            for f in range(2 * k, 2 * k + 2):
                                last = pe.matmul(dense[k][:, (f % 2) * T:(f % 2 + 1) * T],
                                                 wc["L"][:, C_W1 + f * P:C_W1 + (f + 1) * P], xnt[:, 1, s, :],
                                                 start=True, stop=True)
                            last.then_inc(q.c_f1, 1)
                    elif step == "f2":
                        pe.wait_ge(q.c_gelu, NF * (u + 1))
                        dense_job(0, q.c_done, 1, off + BATCH)
                        for t in range(NT):
                            for f in range(NF):
                                last = pe.matmul(dense[0][:, t * D:(t + 1) * D], hid[:, s, f, t * P:(t + 1) * P],
                                                 wc["L"][:, C_W2 + f * D:C_W2 + (f + 1) * D], start=(f == 0),
                                                 stop=(f == NF - 1))
                        last.then_inc(q.c_f2, 1)

            def run(plan):
                read = [None, None]

                def body(n):
                    steps(plan, n, read)
                    for k in range(2):
                        if read[k] is not None:
                            before, per_round, constant = read[k]
                            read[k] = (before, per_round, constant - per_round)

                rounds_of(pe, plan, body)

            pe.wait_ge(s_init, 10)
            pe.wait_ge(s_initv, init_count)
            pe.wait_ge(s_w, 16 * 5)
            run(EXPERT)
            pe.wait_ge(S["F"].c_done, BATCH)
            run(ENCODER)


init_count = 17


def constant_rows():
    slopes = (2.0 ** -(2.0 ** -(np.log2(ENCODER.heads) - 3))) ** np.arange(1, ENCODER.heads + 1)
    slopes = slopes.astype(np.float32)
    bias = (slopes[:, None] * np.arange(T, dtype=np.float32)[None] / np.float32(ENCODER.scale)).astype(np.float32)
    high = (bias.view(np.uint32) & np.uint32(0xFFFFF000)).view(np.float32)
    low = bias - high
    n = P - ALIBI_ROW
    rq = np.zeros((n, GROUPS, ENCODER.hg, T), np.float32)
    rk = np.zeros((n, GROUPS, T), np.float32)
    for i in range(ENCODER.hg):
        for part, b in enumerate((high, low)):
            rq[2 * i + part, :, i, :] = 1.0
            rk[2 * i + part] = b[i::ENCODER.hg]
    rk[n - 1] = 1.0
    rkf = np.zeros((n, GROUPS, T), np.float32)
    rkf[n - 1] = 1.0
    return rq.reshape(n, -1), rk.reshape(n, -1), rkf.reshape(n, -1)


def segments():
    experts = 4
    keep = np.arange(D)[:, None] < (D // 2 ** (np.arange(T) // (T // experts)))[None]
    keep = keep.astype(np.float32)
    return keep, np.ascontiguousarray(keep.T.reshape(NT, P, D).transpose(1, 0, 2))


def kernel(**inputs):
    import concourse.bacc as bacc
    from concourse.bass_utils import run_bass_kernel_spmd

    g = {k: np.asarray(v) for k, v in inputs.items()}

    def rows(v):
        return np.broadcast_to(v[None], (P, v.shape[0]))

    head = np.arange(D).reshape(2, 2, 4, ENCODER.dh)
    v_order = head.transpose(1, 0, 2, 3).reshape(-1)
    o_order = head.transpose(0, 2, 1, 3).reshape(-1)
    def by_stack(plan):
        return np.arange(D).reshape(GROUPS, plan.hg, plan.dh).transpose(1, 2, 0).reshape(-1)

    order, order_f = by_stack(ENCODER), by_stack(EXPERT)
    wa, wc = [], []
    for l in range(LAYERS):
        w, b = g["L0_attn_in_proj_w"][l], g["L0_attn_in_proj_b"][l]
        wa.append(np.concatenate([
            w[0:D][order].T, w[D:2 * D][order].T, w[2 * D:][v_order].T, rows(b[2 * D:][v_order]),
            b[0:D][order][:, None], b[D:2 * D][order][:, None], g["L0_attn_ln1_w"][l][:, None], g["L0_attn_ln1_b"][l][:, None]], 1))
        w2 = g["L0_attn_ffn2_w"][l].T.reshape(NF, P, D).transpose(1, 0, 2).reshape(P, -1)
        wc.append(np.concatenate([
            g["L0_attn_out_proj_w"][l].T[o_order], rows(g["L0_attn_out_proj_b"][l]), g["L0_attn_ffn1_w"][l].T, w2,
            rows(g["L0_attn_ffn2_b"][l]), g["L0_attn_ln2_w"][l][:, None], g["L0_attn_ln2_b"][l][:, None],
            g["L0_attn_ffn1_b"][l].reshape(NF, P).T], 1))
    wa_f = np.concatenate([
        g["L0_ffn_q_w"][order_f].T, g["L0_ffn_k_w"][order_f].T, g["L0_ffn_v_w"].T, rows(g["L0_ffn_v_b"]),
        g["L0_ffn_q_b"][order_f][:, None], g["L0_ffn_k_b"][order_f][:, None], g["L0_ffn_norm_w"][:, None], g["L0_ffn_norm_b"][:, None]], 1)
    wc_f = np.concatenate([g["L0_ffn_o_w"].T, rows(g["L0_ffn_o_b"])], 1)
    fin = np.stack([rows(g["L0_attn_final_w"]), rows(g["L0_attn_final_b"])], 1)
    rq, rk, rkf = constant_rows()
    seg_in, seg_out = segments()
    named = {
        "x": g["L0_attn_x"], "wa_l": np.stack(wa), "wc_l": np.stack(wc), "wa_f": wa_f, "wc_f": wc_f, "fin": fin,
        "rows_q": rq, "rows_k": rk, "rows_kf": rkf, "seg_in": seg_in, "seg_out": seg_out}

    nc = bacc.Bacc("TRN2", target_bir_lowering=False, num_devices=1)
    arrays, args = {}, []
    for name, a in named.items():
        a = np.ascontiguousarray(a)
        arrays[f"in_{name}"] = a
        args.append(nc.dram_tensor(f"in_{name}", a.shape, mybir.dt.from_np(a.dtype), kind="ExternalInput").ap())
    result = nc.dram_tensor("out_0", (BATCH, T, D), F32, kind="ExternalOutput").ap()
    build(nc, *args, result)
    r = run_bass_kernel_spmd(nc, [arrays], core_ids=[0])
    return r.results[0]["out_0"]
```

```python
from contextlib import ExitStack

import numpy as np

import concourse.bass as bass
from concourse import mybir

F32 = mybir.dt.float32
F32R = mybir.dt.float32r
BF16 = mybir.dt.bfloat16
ALU = mybir.AluOpType
ACT = mybir.ActivationFunctionType
AX = mybir.AxisListType

P = 128
BATCH, T, D = 16, 256, 128
NT = T // P
LAYERS, FF = 4, 512
NF = FF // P
EPS = 1e-5
GROUPS = 4
CH = D // GROUPS
COPIES = 3
PARTS = ((0, 0, 1), (0, 1, 0))
ALIBI_ROW = 96
MAX_ROW = 127
MASKED = -1e30
QUARTER = BATCH // 4
OT_BANK = 2

A_Q, A_K, A_V, A_BV, A_BQ, A_BK, A_LNW, A_LNB, A_COLS = 0, 128, 256, 384, 512, 513, 514, 515, 516
C_O, C_BO, C_W1, C_W2, C_B2, C_LNW, C_LNB, C_B1, C_COLS = 0, 128, 256, 768, 1280, 1408, 1409, 1410, 1414
CF_COLS = 256


class Plan:

    def __init__(self, name, heads, causal, feed_forward, rounds):
        self.name, self.heads, self.causal, self.feed_forward, self.rounds = name, heads, causal, feed_forward, rounds
        self.dh = D // heads
        self.hg = heads // GROUPS
        self.scale = float(np.float32((self.dh if causal else D) ** -0.5))
        self.max_chunks = NT * self.hg // 2
        self.exp_chunks = 3 if causal else 2
        self.slot = 16 if causal else 32
        self.stack_dmas = self.hg + 1
        self.units = 2 * rounds

    def slot_steps(self, s, last_layer):
        def at(names, unit):
            return [(name, unit) for name in names.split()]

        ff = self.feed_forward
        maxes = [("max", s + 1, g, ch) for g in range(GROUPS) for ch in range(self.max_chunks)]
        first_exps = [("exp", s, 0, 0), ("exp", s, 0, 1)]
        out = at("ot", s - 1) + at("ln", s + 2) + at("ot+", s - 1) + at("xn", s + 2)
        out = first_exps + out if self.causal else out + first_exps
        out += at("f2 f2+", s - 2) if ff else []
        out += at("at at+", s - 1)
        first_max, more = (2, 2) if self.causal else (4, 1)
        after = [
            at("v v+", s + 1) + at("xt", s + 2),
            at("xt+", s + 2) + at("op", s - 1),
            at("op+", s - 1) + at("qk", s + 2),
            [("pv", s, 0)] + at("qk+", s + 2),
            at("end", s - 2) if last_layer else [],
            at("xn2", s - 1) if ff else [],
            [("pv", s, 1)] + (at("xt2", s - 1) if ff else []),
            at("xt2+", s - 1) if ff else [],
            at("end+", s - 2) if last_layer else [],
            at("negt negt+", s + 1) + [("pv", s, 2)]]
        for k in range(2, 3 * GROUPS):
            g, ch = divmod(k, 3)
            if ch < self.exp_chunks:
                out.append(("exp", s, g, ch))
            if k >= first_max:
                out += maxes[more * (k - first_max):more * (k - first_max + 1)]
            out += after[k - 2]
        out += at("f1 f1+", s - 1) if ff else []
        out += [("pv", s, GROUPS - 1)] + at("pv+", s) + at("stack+", s + 2)
        return out + (at("store", s - 2) if last_layer else [])

    def steps(self, n, last_layer=False):
        for step, off, *g in self.slot_steps(0, last_layer) + self.slot_steps(1, last_layer):
            u = 2 * n + off
            if not isinstance(n, int) or 0 <= u < self.units:
                yield step, u, off % 2, n + off // 2, g, off


EXPERT = Plan("F", 8, False, False, BATCH // 2)
FIRST_END = (LAYERS - 1) * BATCH // 2 + 1
ENCODER = Plan("L", 16, True, True, LAYERS * BATCH // 2)


class Semaphores:

    def __init__(self, sem, name):
        self.a_stats = sem(f"{name}_a_stats")
        self.a_mv = sem(f"{name}_a_mv")
        self.a_eps = sem(f"{name}_a_eps")
        self.a_rstd = sem(f"{name}_a_rstd")
        self.a_xn = sem(f"{name}_a_xn")
        self.a_xt = sem(f"{name}_a_xt")
        self.a_xnt = sem(f"{name}_a_xnt")
        self.a_mask = sem(f"{name}_a_mask")
        self.a_qk = sem(f"{name}_a_qk")
        self.a_v = sem(f"{name}_a_v")
        self.a_y = sem(f"{name}_a_y")
        self.a_hi = sem(f"{name}_a_hi")
        self.a_lo = sem(f"{name}_a_lo")
        self.a_vst = sem(f"{name}_a_vst")
        self.b_max = sem(f"{name}_b_max")
        self.b_red = sem(f"{name}_b_red")
        self.b_nt = sem(f"{name}_b_nt")
        self.b_negt = sem(f"{name}_b_negt")
        self.b_s = sem(f"{name}_b_s")
        self.b_exp = sem(f"{name}_b_exp")
        self.b_pv = sem(f"{name}_b_pv")
        self.c_ost = sem(f"{name}_c_ost")
        self.c_ot = sem(f"{name}_c_ot")
        self.c_rec = sem(f"{name}_c_rec")
        self.c_attn = sem(f"{name}_c_attn")
        self.c_at = sem(f"{name}_c_at")
        self.c_attnt = sem(f"{name}_c_attnt")
        self.c_op = sem(f"{name}_c_op")
        self.c_xb = sem(f"{name}_c_xb")
        self.c_add = sem(f"{name}_c_add")
        self.c_add2 = sem(f"{name}_c_add2")
        self.c_stats = sem(f"{name}_c_stats")
        self.c_mv = sem(f"{name}_c_mv")
        self.c_eps = sem(f"{name}_c_eps")
        self.c_rstd = sem(f"{name}_c_rstd")
        self.c_xn2 = sem(f"{name}_c_xn2")
        self.c_xt2 = sem(f"{name}_c_xt2")
        self.c_xn2t = sem(f"{name}_c_xn2t")
        self.c_f1 = sem(f"{name}_c_f1")
        self.c_gelu = sem(f"{name}_c_gelu")
        self.c_f2 = sem(f"{name}_c_f2")
        self.c_xb2 = sem(f"{name}_c_xb2")
        self.c_done = sem(f"{name}_c_done")
        self.wa = sem(f"{name}_wa")
        self.wc = sem(f"{name}_wc")
        self.wa_ok = sem(f"{name}_wa_ok")
        self.wc_ok = sem(f"{name}_wc_ok")
        self.parts = [sem(f"{name}_parts{s}") for s in range(2)]
        self.stk = [sem(f"{name}_stk{s}") for s in range(2)]
        self.nmax = [sem(f"{name}_nmax{s}") for s in range(2)]


def wait_past(eng, sem, value):
    if isinstance(value, int) and value <= 0:
        return
    eng.wait_ge(sem, value)


def settle(eng, passed):
    eng.sem_inc(passed, 1)


def rounds_of(eng, plan, body):
    body(-1)
    body(0)
    body(1)
    with eng.Fori(2, plan.rounds - 1) as n:
        body(n)
    body(plan.rounds - 1)
    body(plan.rounds)


def encoder_rounds(eng, body):
    body(-1)
    body(0)
    body(1)
    with eng.Fori(2, FIRST_END) as n:
        body(n)
    with eng.Fori(FIRST_END, ENCODER.rounds - 1) as n:
        body(n, last_layer=True)
    body(ENCODER.rounds - 1, last_layer=True)
    body(ENCODER.rounds, last_layer=True)


def build(nc, x_in, wa_l, wc_l, wa_f, wc_f, fin_w, rows_q, rows_k, rows_kf, seg_in, seg_out, out):
    with ExitStack() as ctx:
        def sb(name, shape, dt=F32):
            return ctx.enter_context(nc.sbuf_tensor(name, shape, dt))

        def ps(name, shape):
            return ctx.enter_context(nc.psum_tensor(name, shape, F32))

        def sem(name):
            return ctx.enter_context(nc.semaphore(name))

        state = sb("state", [P, BATCH, NT, D])
        rest = sb("rest", [P, BATCH, NT, D])
        wa = {"F": sb("wa_f", [P, A_COLS]), "L": sb("wa_l", [P, A_COLS])}
        wc = {"F": sb("wc_f", [P, CF_COLS]), "L": sb("wc_l", [P, C_COLS])}
        fin = sb("fin", [P, 2, D])
        seg_rows = sb("seg_rows", [P, T])
        seg_cols = sb("seg_cols", [P, NT, D])
        qbd = {"L": sb("qbd_l", [P, 2, ENCODER.heads, T], F32R), "F": sb("qbd_f", [P, 2, EXPERT.heads, T], F32R)}
        kst = {"L": sb("kst_l", [P, 2, GROUPS, T], F32R), "F": sb("kst_f", [P, 2, GROUPS, T], F32R)}
        probs = sb("probs", [P, GROUPS, 3, 512])
        vst = {"L": sb("vst_l", [P, 2, NT, 2, 8, 32]), "F": sb("vst_f", [P, 2, NT, 1, 8, 32])}
        stats = sb("stats", [P, 3, 2, NT, 6])
        mv = sb("mv", [P, 3, 2, NT, 2])
        veps = sb("veps", [P, 3, 2, NT])
        rstd = sb("rstd", [P, 3, 2, NT])
        stats_all = sb("stats_all", [P, BATCH * NT, 6])
        mv_all = sb("mv_all", [P, BATCH * NT, 2])
        veps_all = sb("veps_all", [P, BATCH * NT])
        rstd_all = sb("rstd_all", [P, BATCH * NT])
        half = sb("half", [P, BATCH * NT])
        xn = sb("xn", [P, 2, 2, NT, D])
        xnt = sb("xnt", [P, 2, 2, T])
        y = sb("y", [P, 2, 2 * T])
        hi = sb("hi", [P, 2, 2 * T], F32R)
        lo = sb("lo", [P, 2, 2 * T], F32R)
        negm = sb("negm", [P, 2, NT, 16])
        negt = sb("negt", [16, 2, NT, P], F32R)
        ost = sb("ost", [P, 2, 2, T])
        rec = sb("rec", [P, 2, 32])
        attn = sb("attn", [P, 2, NT, D])
        attnt = sb("attnt", [P, 2, T])
        xb = sb("xb", [P, 2, NT, D])
        xb2 = sb("xb2", [P, 2, NT, D])
        tmp = sb("tmp", [P, 2, NT, D])
        hid = sb("hid", [P, 2, NF, T])
        fo = sb("fo", [P, 2, NT, D])
        ident = sb("ident", [P, P])
        identb = sb("identb", [P, P], BF16)
        maskf = sb("maskf", [P, 2, P])
        maskb = sb("maskb", [P, 2, P], BF16)
        masktf = sb("masktf", [P, 4, P])
        masktb = sb("masktb", [P, 4, P], BF16)

        split = {p.name: nc.dram_tensor(f"split_{p.name}", [2, 2, p.hg, COPIES, p.dh, GROUPS * T], F32,
                                        kind="Internal").ap() for p in (EXPERT, ENCODER)}

        dense = [ps("dense0", [P, 512]), ps("dense1", [P, 512])]
        mxp = ps("mxp", [P, 3, 512])
        exp_ps = ps("exp_ps", [P, 2, 512])
        pvp = ps("pvp", [P, 512])

        s_x = [sem(f"s_x{k}") for k in range(4)]
        s_w = sem("s_w")
        s_init = sem("s_init")
        s_zero = sem("s_zero")
        s_initv = sem("s_initv")
        s_rows = sem("s_rows")
        s_rounded = sem("s_rounded")
        s_stats = sem("s_stats")
        s_mv = sem("s_mv")
        s_eps = sem("s_eps")
        s_rstd = sem("s_rstd")
        s_norm = sem("s_norm")
        s_end_stats = sem("s_end_stats")
        s_end_mv = sem("s_end_mv")
        s_end_eps = sem("s_end_eps")
        s_end_rstd = sem("s_end_rstd")
        s_end_rest = sem("s_end_rest")
        s_end_norm = sem("s_end_norm")
        s_end_scaled = sem("s_end_scaled")
        s_final = sem("s_final")
        s_store = [sem(f"s_store{s}") for s in range(2)]
        passed_dve, passed_pool, passed_sp = sem("passed_dve"), sem("passed_pool"), sem("passed_sp")
        S = {p.name: Semaphores(sem, p.name) for p in (EXPERT, ENCODER)}

        in_rows = probs[ALIBI_ROW:P, :, :, :].rearrange("p a b c -> p (a b c)")
        k_row, q_row = GROUPS * T, ENCODER.heads * T
        constant = [in_rows[:, 0:k_row], in_rows[:, k_row:2 * k_row], in_rows[:, 2 * k_row:2 * k_row + q_row]]

        block = ctx.enter_context(nc.Block())

        @block.sync
        def _(sp):
            xv = x_in.rearrange("b (t p) d -> p b t d", p=P)
            for k in range(4):
                sp.dma_start(rest[:, 4 * k:4 * k + 4, :, :], xv[:, 4 * k:4 * k + 4, :, :]).then_inc(s_x[k], 16)
            for dst, src in ((wa["F"], wa_f), (wc["F"], wc_f), (fin, fin_w), (seg_rows, seg_in), (seg_cols, seg_out)):
                sp.dma_start(dst[:], src).then_inc(s_w, 16)
            for dst, src in zip(constant, (rows_kf, rows_k, rows_q)):
                sp.dma_start(dst, src).then_inc(s_rows, 16)

            def keep_parts(plan, q, u, r, s):
                wait_past(sp, q.stk[s], 16 * plan.stack_dmas * r)
                settle(sp, passed_sp)
                for part, ready, source in ((0, q.a_hi, hi), (1, q.a_lo, lo)):
                    sp.wait_ge(ready, u + 1)
                    for qk in range(2):
                        for copy in range(COPIES):
                            if PARTS[qk][copy] == part:
                                dst = split[plan.name][s, qk, :, copy].rearrange("i d (g t) -> i (d g) t", t=T)
                                sp.dma_start(dst, source[:, s, qk * T:(qk + 1) * T].bitcast(F32)).then_inc(q.parts[s], 16)

            def stack_queries_and_keys(plan, q, u, r, s):
                sc = split[plan.name][s]
                sp.wait_ge(q.parts[s], 16 * 2 * COPIES * (r + 1))
                settle(sp, passed_sp)
                wait_past(sp, q.b_s, plan.exp_chunks * GROUPS * (u - 1))
                settle(sp, passed_sp)
                rows = COPIES * plan.dh
                sp.dma_start(kst[plan.name][0:plan.hg * rows, s, :, :].bitcast(F32),
                             sc[1].rearrange("i c d (g t) -> (i c d) g t", t=T)).then_inc(q.stk[s], 16)
                qd = qbd[plan.name][:, s].bitcast(F32).rearrange("p (g i) t -> p g i t", g=GROUPS)
                for i in range(plan.hg):
                    sp.dma_start(qd[i * rows:(i + 1) * rows, :, i, :],
                                 sc[0, i].rearrange("c d (g t) -> (c d) g t", t=T)).then_inc(q.stk[s], 16)

            def share(plan, q, step, u, s, r):
                if step == "qk+":
                    keep_parts(plan, q, u, r, s)
                elif step == "stack+":
                    stack_queries_and_keys(plan, q, u, r, s)
                elif step == "negt+":
                    sp.wait_ge(q.b_negt, u + 1)
                    sp.dma_start(qbd[plan.name][MAX_ROW:MAX_ROW + 1, s, :, :].bitcast(F32),
                                 negt[0:plan.heads, s, :, :].bitcast(F32)).then_inc(q.nmax[s], 16)

            def expert_round(n):
                for step, u, s, r, *_ in EXPERT.steps(n):
                    share(EXPERT, S["F"], step, u, s, r)

            rounds_of(sp, EXPERT, expert_round)

            q, per = S["L"], BATCH // 2
            sp.dma_start(wa["L"][:], wa_l[0]).then_inc(q.wa, 16)
            sp.wait_ge(S["F"].c_done, BATCH)
            sp.wait_ge(q.wa, 16)

            def load_a(layer):
                sp.wait_ge(q.a_vst, BATCH * layer)
                settle(sp, passed_sp)
                sp.dma_start(wa["L"][:], wa_l[layer]).then_inc(q.wa, 16)
                sp.wait_ge(q.wa, 16 * (layer + 1))
                settle(sp, passed_sp)

            def load_c(layer):
                sp.wait_ge(q.c_done, BATCH * (layer + 1))
                settle(sp, passed_sp)
                sp.dma_start(wc["L"][:], wc_l[layer]).then_inc(q.wc, 16)
                sp.wait_ge(q.wc, 16 * (layer + 1))
                settle(sp, passed_sp)

            ov = out.rearrange("b (t p) d -> b p t d", p=P)

            def encoder_round(n, first_of=None, last_of=None, last_layer=False):
                for step, u, s, r, *_ in ENCODER.steps(n, last_layer):
                    share(ENCODER, q, step, u, s, r)
                    if step == "store":
                        b = u - (LAYERS - 1) * BATCH
                        sp.wait_ge(s_final, b + 3)
                        settle(sp, passed_sp)
                        sp.dma_start(ov[b], fo[:, s, :, :]).then_inc(s_store[s], 16)
                    if step == "xt" and s == 0:
                        if last_of is not None:
                            load_a(last_of + 1)
                        sp.sem_inc(q.wa_ok, 1)
                    if step == "op":
                        if first_of is not None and s == 0:
                            load_c(first_of)
                        sp.sem_inc(q.wc_ok, 1)

            def layer_rounds(layer, last=False):
                with sp.Fori(1, per - 1) as j:
                    encoder_round(per * layer + j, last_layer=last)
                encoder_round(per * layer + per - 1, last_of=None if last else layer, last_layer=last)

            encoder_round(-1)
            encoder_round(0, first_of=0)
            encoder_round(1)
            with sp.Fori(2, per - 1) as j:
                encoder_round(j)
            encoder_round(per - 1, last_of=0)
            with sp.Fori(1, LAYERS - 1) as layer:
                encoder_round(per * layer, first_of=layer)
                layer_rounds(layer)
            encoder_round(per * (LAYERS - 1), first_of=LAYERS - 1)
            layer_rounds(LAYERS - 1, last=True)
            encoder_round(per * LAYERS, last_layer=True)

            for s in range(2):
                sp.wait_ge(s_store[s], 16 * (BATCH // 2 + 1))

        @block.gpsimd
        def _(pool):
            pool.memset(ident[:], 0.0).then_inc(s_init, 1)
            pool.memset(maskf[:], 0.0).then_inc(s_init, 1)
            pool.memset(half[:], -0.5).then_inc(s_init, 1)
            pool.memset(masktf[:], 0.0).then_inc(s_init, 1)
            pool.wait_ge(s_init, 4)
            pool.affine_select(out=ident[:], in_=ident[:], compare_op=ALU.not_equal, fill=1.0, base=0,
                               pattern=[[-1, P]], channel_multiplier=1).then_inc(s_init, 1)
            pool.affine_select(out=maskf[:], in_=maskf[:], compare_op=ALU.is_ge, fill=MASKED, base=0,
                               pattern=[[0, 2], [-1, P]], channel_multiplier=1).then_inc(s_init, 1)
            pool.affine_select(out=masktf[:], in_=masktf[:], compare_op=ALU.is_ge, fill=MASKED, base=0,
                               pattern=[[0, 4], [1, P]], channel_multiplier=-1).then_inc(s_init, 1)
            pool.wait_ge(s_init, 7)
            pool.tensor_copy(identb[:], ident[:]).then_inc(s_init, 1)
            pool.tensor_copy(maskb[:], maskf[:]).then_inc(s_init, 1)
            pool.tensor_copy(masktb[:], masktf[:]).then_inc(s_init, 1)

            def inverse_deviation_of_quarter(k, count):
                rows_ = slice(k * QUARTER * NT, (k + 1) * QUARTER * NT)
                pool.wait_ge(s_mv, count)
                pool.tensor_scalar(veps_all[:, rows_], mv_all[:, rows_, 1], EPS, None, ALU.add).then_inc(s_eps, 1)
                pool.wait_ge(s_eps, count)
                pool.tensor_tensor(rstd_all[:, rows_], veps_all[:, rows_], half[:, rows_], ALU.pow).then_inc(s_rstd, 1)

            def inverse_deviation(q, stage, u, s):
                k = "AC".index(stage)
                ready, eps, done = (q.a_mv, q.a_eps, q.a_rstd) if stage == "A" else (q.c_mv, q.c_eps, q.c_rstd)
                pool.wait_ge(ready, u + 1)
                settle(pool, passed_pool)
                pool.tensor_scalar(veps[:, k, s, :], mv[:, k, s, :, 1], EPS, None, ALU.add).then_inc(eps, 1)
                pool.wait_ge(eps, u + 1)
                pool.tensor_tensor(rstd[:, k, s, :], veps[:, k, s, :], half[:, 0:NT], ALU.pow).then_inc(done, 1)

            def steps(plan, n, last_layer=False):
                q = S[plan.name]
                for step, u, s, r, g, _ in plan.steps(n, last_layer):
                    if step == "ln":
                        inverse_deviation(q, "A", u, s)
                    elif step == "end":
                        b = u - (LAYERS - 1) * BATCH
                        pool.wait_ge(s_end_mv, b + 1)
                        settle(pool, passed_pool)
                        pool.tensor_scalar(veps[:, 2, s, :], mv[:, 2, s, :, 1], EPS, None, ALU.add).then_inc(s_end_eps, 1)
                        pool.wait_ge(s_end_eps, b + 1)
                        settle(pool, passed_pool)
                        pool.tensor_tensor(rstd[:, 2, s, :], veps[:, 2, s, :], half[:, 0:NT], ALU.pow)\
                            .then_inc(s_end_rstd, 1)
                        bias = fin[:, 1, :].unsqueeze(1).to_broadcast([P, NT, D])
                        pool.tensor_tensor(rest[:, b, :, :], rest[:, b, :, :], bias, ALU.add).then_inc(s_end_rest, 1)
                    elif step == "end+":
                        b = u - (LAYERS - 1) * BATCH
                        weight = fin[:, 0, :].unsqueeze(1).to_broadcast([P, NT, D])
                        pool.wait_ge(s_end_norm, b + 1)
                        settle(pool, passed_pool)
                        pool.tensor_tensor(tmp[:, s, :, :], tmp[:, s, :, :], weight, ALU.mult).then_inc(s_end_scaled, 1)
                        pool.wait_ge(s_end_scaled, b + 1)
                        pool.wait_ge(s_end_rest, b + 1)
                        pool.wait_ge(s_store[s], 16 * (b // 2 + 1))
                        settle(pool, passed_pool)
                        pool.tensor_tensor(fo[:, s, :, :], tmp[:, s, :, :], rest[:, b, :, :], ALU.add).then_inc(s_final, 1)
                    elif step == "qk+":
                        pool.wait_ge(q.a_hi, u + 1)
                        wait_past(pool, q.parts[s], 16 * 2 * COPIES * r)
                        pool.tensor_tensor(lo[:, s, :], y[:, s, :], hi[:, s, :].bitcast(F32), ALU.subtract)\
                            .then_inc(q.a_lo, 1)
                    elif step == "op":
                        if plan.causal:
                            bt = u % BATCH
                            pool.wait_ge(q.c_done, u + 1)
                            pool.wait_ge(q.wc_ok, u + 1)
                            wait_past(pool, q.c_add, u - 1)
                            settle(pool, passed_pool)
                            for t in range(NT):
                                last = pool.tensor_tensor(xb[:, s, t, :], state[:, bt, t, :], wc["L"][:, C_BO:C_BO + D], ALU.add)
                            last.then_inc(q.c_xb, 1)
                        else:
                            pool.wait_ge(s_norm, u + 1)
                            wait_past(pool, q.c_done, u - 1)
                            settle(pool, passed_pool)
                            pool.tensor_tensor(xb[:, s, :, :], state[:, u, :, :], rest[:, u, :, :], ALU.add)\
                                .then_inc(q.c_xb, 1)
                    elif step == "op+" and plan.feed_forward:
                        inverse_deviation(q, "C", u, s)
                        wait_past(pool, q.c_done, BATCH + u - 1)
                        settle(pool, passed_pool)
                        for t in range(NT):
                            last = pool.tensor_tensor(xb2[:, s, t, :], state[:, u % BATCH, t, :], wc["L"][:, C_B2:C_B2 + D], ALU.add)
                        last.then_inc(q.c_xb2, 1)

            pool.memset(qbd["F"][:].bitcast(F32), 0.0).then_inc(s_zero, 1)
            pool.memset(vst["F"][:], 0.0).then_inc(s_zero, 1)
            pool.memset(vst["L"][:], 0.0).then_inc(s_zero, 1)
            pool.wait_ge(s_zero, 3)
            pool.memset(vst["F"][:, :, :, :, :, 16:17], 1.0).then_inc(s_init, 1)
            pool.memset(vst["L"][:, :, :, 0, :, 8:9], 1.0).then_inc(s_init, 1)
            pool.memset(vst["L"][:, :, :, 1, :, 24:25], 1.0).then_inc(s_init, 1)
            for k in range(4):
                inverse_deviation_of_quarter(k, k + 1)
            pool.wait_ge(s_w, 16 * 5)
            rounds_of(pool, EXPERT, lambda n: steps(EXPERT, n))
            pool.wait_ge(S["F"].c_done, BATCH)
            pool.sem_inc(s_final, 2)
            for s in range(2):
                pool.sem_inc(s_store[s], 16)
            encoder_rounds(pool, lambda n, last_layer=False: steps(ENCODER, n, last_layer))

        @block.vector
        def _(dve):
            dve.memset(qbd["L"][0:ALIBI_ROW, :, :, :].bitcast(F32), 0.0).then_inc(s_initv, 1)

            def statistics_of_quarter(source, k, count):
                rows_ = range(k * QUARTER * NT, (k + 1) * QUARTER * NT)
                for r in rows_:
                    last = dve.bn_stats(stats_all[:, r, :], source[:, r // NT, r % NT, :])
                last.then_inc(s_stats, 1)
                dve.wait_ge(s_stats, count)
                settle(dve, passed_dve)
                for r in rows_:
                    last = dve.bn_aggr(mv_all[:, r, :], stats_all[:, r, :])
                last.then_inc(s_mv, 1)

            def first_norm(k):
                dve.wait_ge(s_rstd, k + 1)
                for b in range(k * QUARTER, (k + 1) * QUARTER):
                    for t in range(NT):
                        r = b * NT + t
                        last = dve.tensor_scalar(state[:, b, t, :], rest[:, b, t, :], mv_all[:, r, 0:1],
                                                 rstd_all[:, r:r + 1], ALU.subtract, ALU.mult)
                    last.then_inc(s_norm, 1)

            for k in range(4):
                dve.wait_ge(s_x[k], 16)
                settle(dve, passed_dve)
                statistics_of_quarter(rest, k, k + 1)
                if k:
                    first_norm(k - 1)
            first_norm(3)
            dve.wait_ge(s_w, 16 * 5)

            def statistics(q, stage, u, s, source):
                k = "AC".index(stage)
                done, ready = (q.a_stats, q.a_mv) if stage == "A" else (q.c_stats, q.c_mv)
                settle(dve, passed_dve)
                for t in range(NT):
                    last = dve.bn_stats(stats[:, k, s, t, :], source[:, t, :])
                last.then_inc(done, 1)
                dve.wait_ge(done, u + 1)
                settle(dve, passed_dve)
                for t in range(NT):
                    last = dve.bn_aggr(mv[:, k, s, t, :], stats[:, k, s, t, :])
                last.then_inc(ready, 1)

            def normalise(q, stage, u, s, source):
                k = "AC".index(stage)
                rstd_ready, used, done = (q.a_rstd, q.a_xt, q.a_xn) if stage == "A" else (q.c_rstd, q.c_xt2, q.c_xn2)
                dve.wait_ge(rstd_ready, u + 1)
                wait_past(dve, used, u - 1)
                for t in range(NT):
                    last = dve.tensor_scalar(xn[:, k, s, t, :], source[:, t, :], mv[:, k, s, t, 0:1],
                                             rstd[:, k, s, t:t + 1], ALU.subtract, ALU.mult)
                last.then_inc(done, 1)

            def high_parts(q, u, r, s):
                dve.wait_ge(q.a_y, 2 * (u + 1))
                wait_past(dve, q.parts[s], 16 * 2 * COPIES * r)
                dve.tensor_copy(hi[:, s, :], y[:, s, :]).then_inc(q.a_hi, 1)

            def place_values(plan, q, u, s):
                dve.wait_ge(q.a_v, u + 1)
                wait_past(dve, q.b_pv, GROUPS * (u - 1))
                bias = wa[plan.name][:, A_BV:A_BV + D]
                halves = 2 if plan.causal else 1
                for h in range(halves):
                    width = D // halves
                    for t in range(NT):
                        i0 = dense[0][:, t * D + h * width:t * D + (h + 1) * width].rearrange("p (h d) -> p h d", d=plan.dh)
                        i1 = bias[:, h * width:(h + 1) * width].rearrange("p (h d) -> p h d", d=plan.dh)
                        o = vst[plan.name][:, s, t, h, :, plan.slot * h:plan.slot * h + plan.dh]
                        last = dve.tensor_tensor(o, i0, i1, ALU.add)
                last.then_inc(q.a_vst, 1)

            def maxima(plan, q, u, s, g, ch):
                c = plan.max_chunks * (GROUPS * u + g) + ch
                qt, pair = ch % NT, ch // NT
                dve.wait_ge(q.b_max, c + 1)
                if g == 0 and ch == 0:
                    wait_past(dve, q.b_nt, u - 1)
                keys = P if plan.causal and qt == 0 else T
                h0 = plan.hg * g + 2 * pair
                dve.tensor_reduce(negm[:, s, qt, h0:h0 + 2],
                                  mxp[:, (plan.max_chunks * g + ch) % 3, :].rearrange("p (h t) -> p h t", h=2)[:, :, 0:keys],
                                  AX.X, ALU.max, negate=True).then_inc(q.b_red, 1)

            def divide_by_sums(plan, q, u, s):
                slots = P // plan.slot * 4
                v = mxp[:, OT_BANK, :].rearrange("p (a c) -> p a c", c=plan.slot)
                dve.wait_ge(q.c_ot, u + 1)
                dve.reciprocal(rec[:, s, 0:slots], v[:, :, plan.dh]).then_inc(q.c_rec, 1)
                dve.wait_ge(q.c_rec, u + 1)
                wait_past(dve, q.c_at, u - 1)
                r = rec[:, s, 0:slots].unsqueeze(2).to_broadcast([P, slots, plan.dh])
                o = attn[:, s, :, :].rearrange("p t (a d) -> p (t a) d", d=plan.dh)
                dve.tensor_tensor(o, v[:, :, 0:plan.dh], r, ALU.mult).then_inc(q.c_attn, 1)

            def steps(plan, n, last_layer=False):
                q = S[plan.name]
                for step, u, s, r, g, _ in plan.steps(n, last_layer):
                    bt = u % BATCH if plan.causal else u
                    if step == "ln":
                        if plan.causal:
                            dve.wait_ge(q.c_done, u + 1)
                        else:
                            dve.wait_ge(s_norm, u + 1)
                        statistics(q, "A", u, s, state[:, bt])
                    elif step == "xn":
                        normalise(q, "A", u, s, state[:, bt])
                    elif step == "xt+" and not plan.causal:
                        dve.wait_ge(q.a_xnt, u + 1)
                        dve.tensor_tensor(xnt[:, 0, s, :], xnt[:, 0, s, :], seg_rows[:], ALU.mult).then_inc(q.a_mask, 1)
                    elif step == "qk+":
                        high_parts(q, u, r, s)
                    elif step == "v+":
                        place_values(plan, q, u, s)
                    elif step == "max":
                        maxima(plan, q, u, s, *g)
                    elif step == "negt+":
                        dve.wait_ge(q.b_nt, u + 1)
                        wait_past(dve, q.nmax[s], 16 * r)
                        dve.tensor_copy(negt[0:plan.heads, s, :, :],
                                        dense[1][0:plan.heads, 0:T].rearrange("p (t c) -> p t c", t=NT))\
                           .then_inc(q.b_negt, 1)
                    elif step == "pv+":
                        dve.wait_ge(q.b_pv, GROUPS * (u + 1))
                        wait_past(dve, q.c_ot, u - 1)
                        dve.tensor_copy(ost[:, s, :, :].rearrange("p r t -> p (r t)"), pvp[:, :]).then_inc(q.c_ost, 1)
                    elif step == "ot+":
                        divide_by_sums(plan, q, u, s)
                    elif step == "at+" and not plan.causal:
                        dve.wait_ge(q.c_at, u + 1)
                        wait_past(dve, q.c_op, u - 1)
                        dve.tensor_tensor(attnt[:, s, :], dense[1][:, 0:T], seg_rows[:], ALU.mult).then_inc(q.c_attnt, 1)
                    elif step == "op+":
                        projected = dense[0][:, 0:T].rearrange("p (t d) -> p t d", t=NT)
                        dve.wait_ge(q.c_op, u + 1)
                        if plan.feed_forward:
                            dve.wait_ge(q.c_xb, u + 1)
                            dve.tensor_tensor(state[:, bt, :, :], projected, xb[:, s, :, :], ALU.add).then_inc(q.c_add, 1)
                            dve.wait_ge(q.c_add, u + 1)
                            statistics(q, "C", u, s, state[:, bt])
                        else:
                            bias = wc["F"][:, C_BO:C_BO + D].unsqueeze(1).to_broadcast([P, NT, D])
                            dve.tensor_tensor(tmp[:, s, :, :], projected, bias, ALU.add).then_inc(q.c_add, 1)
                            dve.wait_ge(q.c_add, u + 1)
                            dve.tensor_tensor(tmp[:, s, :, :], tmp[:, s, :, :], seg_cols[:], ALU.mult).then_inc(q.c_add2, 1)
                            dve.wait_ge(q.c_add2, u + 1)
                            dve.wait_ge(q.c_xb, u + 1)
                            dve.tensor_tensor(rest[:, bt, :, :], tmp[:, s, :, :], xb[:, s, :, :], ALU.add).then_inc(q.c_done, 1)
                    elif step == "end":
                        b = u - (LAYERS - 1) * BATCH
                        dve.wait_ge(q.c_done, BATCH + u + 1)
                        settle(dve, passed_dve)
                        for t in range(NT):
                            last = dve.bn_stats(stats[:, 2, s, t, :], state[:, b, t, :])
                        last.then_inc(s_end_stats, 1)
                        dve.wait_ge(s_end_stats, b + 1)
                        settle(dve, passed_dve)
                        for t in range(NT):
                            last = dve.bn_aggr(mv[:, 2, s, t, :], stats[:, 2, s, t, :])
                        last.then_inc(s_end_mv, 1)
                    elif step == "end+":
                        b = u - (LAYERS - 1) * BATCH
                        dve.wait_ge(s_end_rstd, b + 1)
                        dve.wait_ge(s_final, b + 1)
                        for t in range(NT):
                            last = dve.tensor_scalar(tmp[:, s, t, :], state[:, b, t, :], mv[:, 2, s, t, 0:1],
                                                     rstd[:, 2, s, t:t + 1], ALU.subtract, ALU.mult)
                        last.then_inc(s_end_norm, 1)
                    elif step == "xn2":
                        normalise(q, "C", u, s, state[:, bt])
                    elif step == "f2+":
                        dve.wait_ge(q.c_f2, u + 1)
                        dve.wait_ge(q.c_xb2, u + 1)
                        dve.tensor_tensor(state[:, bt, :, :], dense[0][:, 0:T].rearrange("p (t d) -> p t d", t=NT),
                                          xb2[:, s, :, :], ALU.add).then_inc(q.c_done, 1)

            rounds_of(dve, EXPERT, lambda n: steps(EXPERT, n))
            dve.wait_ge(S["F"].c_done, BATCH)
            dve.memset(rec[:, 0, 0:1], 0.0).then_inc(S["L"].c_done, BATCH)
            encoder_rounds(dve, lambda n, last_layer=False: steps(ENCODER, n, last_layer))

        @block.scalar
        def _(act):
            act.wait_ge(s_rows, 16 * 3)
            for s in range(2):
                for stack, source in zip((kst["F"], kst["L"], qbd["L"]), constant):
                    act.activation(stack[ALIBI_ROW:P, s, :, :].rearrange("p h t -> p (h t)"), source, ACT.Copy)\
                       .then_inc(s_rounded, 1)
            act.wait_ge(s_w, 16 * 5)

            def steps(plan, n):
                q = S[plan.name]
                for step, u, s, r, g, _ in plan.steps(n):
                    if step == "xt+":
                        w = wa[plan.name]
                        act.wait_ge(q.a_xt, u + 1)
                        wait_past(act, q.a_v, u - 1)
                        act.activation(xnt[:, 0, s, :], dense[1][:, 0:T], ACT.Identity, bias=w[:, A_LNB:A_LNB + 1],
                                       scale=w[:, A_LNW:A_LNW + 1]).then_inc(q.a_xnt, 1)
                    elif step == "qk+":
                        w = wa[plan.name]
                        act.wait_ge(q.a_qk, u + 1)
                        wait_past(act, q.a_lo, u - 1)
                        for k, col in enumerate((A_BQ, A_BK)):
                            act.activation(y[:, s, k * T:(k + 1) * T], dense[1][:, k * T:(k + 1) * T], ACT.Identity,
                                           bias=w[:, col:col + 1]).then_inc(q.a_y, 1)
                    elif step == "exp":
                        G, ch = GROUPS * u + g[0], g[1]
                        if ch == 0:
                            wait_past(act, q.b_pv, G - GROUPS + 1)
                        act.wait_ge(q.b_s, plan.exp_chunks * G + ch + 1)
                        act.activation(probs[:, g[0], ch, :], exp_ps[:, (plan.exp_chunks * g[0] + ch) % 2, :], ACT.Exp,
                                       scale=plan.scale).then_inc(q.b_exp, 1)
                    elif step == "at+" and plan.causal:
                        act.wait_ge(q.c_at, u + 1)
                        wait_past(act, q.c_op, u - 1)
                        act.activation(attnt[:, s, :], dense[1][:, 0:T], ACT.Copy).then_inc(q.c_attnt, 1)
                    elif step == "xt2+":
                        w = wc["L"]
                        act.wait_ge(q.c_xt2, u + 1)
                        wait_past(act, q.c_f1, 2 * (u - 1))
                        act.activation(xnt[:, 1, s, :], dense[0][:, 0:T], ACT.Identity, bias=w[:, C_LNB:C_LNB + 1],
                                       scale=w[:, C_LNW:C_LNW + 1]).then_inc(q.c_xn2t, 1)
                    elif step == "f1+":
                        wait_past(act, q.c_f2, u - 1)
                        for f in range(NF):
                            if f % 2 == 0:
                                act.wait_ge(q.c_f1, 2 * u + f // 2 + 1)
                            act.activation(hid[:, s, f, :], dense[f // 2][:, (f % 2) * T:(f % 2 + 1) * T], ACT.Gelu,
                                           bias=wc["L"][:, C_B1 + f:C_B1 + f + 1]).then_inc(q.c_gelu, 1)

            rounds_of(act, EXPERT, lambda n: steps(EXPERT, n))
            act.wait_ge(S["F"].c_done, BATCH)
            rounds_of(act, ENCODER, lambda n: steps(ENCODER, n))

        @block.tensor
        def _(pe):
            def transposes(out_bank, sources, done):
                for k, src in enumerate(sources):
                    width = src.shape[0]
                    last = pe.transpose(out_bank[0:src.shape[1], k * width:(k + 1) * width], src, ident[:, :])
                last.then_inc(done, 1)

            def steps(plan, n, read):
                q = S[plan.name]

                def dense_job(bank, sem, count, unit_offset):
                    if read[bank] is not None:
                        before, per_round, constant = read[bank]
                        pe.wait_ge(before, per_round * n + constant)
                    read[bank] = (sem, 2 * count, count * (unit_offset + 1))

                for step, u, s, r, g, off in plan.steps(n):
                    if step == "xt":
                        if plan.causal:
                            pe.wait_ge(q.wa_ok, n + 2)
                        pe.wait_ge(q.a_xn, u + 1)
                        dense_job(1, q.a_xnt, 1, off)
                        transposes(dense[1], [xn[:, 0, s, t, :] for t in range(NT)], q.a_xt)
                    elif step == "qk":
                        w = wa[plan.name]
                        pe.wait_ge(q.a_xnt if plan.causal else q.a_mask, u + 1)
                        dense_job(1, q.a_y, 2, off)
                        for k, col in enumerate((A_Q, A_K)):
                            last = pe.matmul(dense[1][:, k * T:(k + 1) * T], w[:, col:col + D], xnt[:, 0, s, :],
                                             start=True, stop=True)
                        last.then_inc(q.a_qk, 1)
                    elif step == "v":
                        w = wa[plan.name]
                        dense_job(0, q.a_vst, 1, off)
                        for t in range(NT):
                            last = pe.matmul(dense[0][:, t * D:(t + 1) * D], xnt[:, 0, s, t * P:(t + 1) * P],
                                             w[:, A_V:A_V + D], start=True, stop=True)
                        last.then_inc(q.a_v, 1)
                    elif step == "max":
                        ch = g[1]
                        if g == [0, 0]:
                            pe.wait_ge(q.stk[s], 16 * plan.stack_dmas * (r + 1))
                        k_unit = plan.max_chunks * g[0] + ch
                        bank = k_unit % 3
                        if k_unit >= 3:
                            pe.wait_ge(q.b_red, plan.max_chunks * GROUPS * u + k_unit - 2)
                        if k_unit == OT_BANK:
                            wait_past(pe, q.c_attn, u - 1)
                        qt, pair = ch % NT, ch // NT
                        for k in range(2):
                            h = plan.hg * g[0] + 2 * pair + k
                            last = pe.matmul(mxp[:, bank, k * T:(k + 1) * T],
                                             qbd[plan.name][0:MAX_ROW, s, h, qt * P:(qt + 1) * P],
                                             kst[plan.name][0:MAX_ROW, s, g[0], :],
                                             start=(k == 0), stop=True, skip_group_check=True)
                        if plan.causal:
                            o = mxp[:, bank, :].rearrange("p (h t) -> p h t", h=2)[:, :, qt * P:(qt + 1) * P]
                            last = pe.matmul(o, identb[:, :], maskb[:, :, :], start=False, stop=True,
                                             skip_group_check=True)
                        last.then_inc(q.b_max, 1)
                    elif step == "negt":
                        pe.wait_ge(q.b_red, GROUPS * plan.max_chunks * (u + 1))
                        dense_job(1, q.b_negt, 1, off)
                        transposes(dense[1], [negm[:, s, t, 0:plan.heads] for t in range(NT)], q.b_nt)
                    elif step == "exp":
                        ch, h0 = g[1], plan.hg * g[0]
                        if g == [0, 0]:
                            pe.wait_ge(q.nmax[s], 16 * (r + 1))
                        bank = (plan.exp_chunks * g[0] + ch) % 2
                        wait_past(pe, q.b_exp, plan.exp_chunks * (GROUPS * u + g[0]) + ch - 1)
                        if not plan.causal:
                            kt, rhs = ch, qbd["F"][:, s, h0:h0 + 2, :]
                        elif ch < 2:
                            kt, rhs = 0, qbd["L"][:, s, h0 + 2 * ch:h0 + 2 * ch + 2, :]
                        else:
                            kt, rhs = 1, qbd["L"][:, s, h0:h0 + 4, P:T]
                        last = pe.matmul(exp_ps[:, bank, :], kst[plan.name][:, s, g[0], kt * P:(kt + 1) * P], rhs,
                                         start=True, stop=True, skip_group_check=True)
                        if plan.causal:
                            heads = 4 if kt else 2
                            o = exp_ps[:, bank, :].rearrange("p (h t) -> p h t", h=heads)[:, :, 0:P]
                            last = pe.matmul(o, identb[:, :], masktb[:, 0:heads, :], start=False, stop=True,
                                             skip_group_check=True)
                        last.then_inc(q.b_s, 1)
                    elif step == "pv":
                        G = GROUPS * u + g[0]
                        if g[0] == 0:
                            pe.wait_ge(q.a_vst, u + 1)
                            wait_past(pe, q.c_ost, u)
                        pe.wait_ge(q.b_exp, plan.exp_chunks * (G + 1))
                        region, half_ = g[0] // 2, g[0] % 2
                        for kt in range(NT):
                            for i in range(plan.hg):
                                if plan.causal:
                                    col, lead = i, half_ == 0 and kt == 0
                                    q0 = P * kt
                                    src = (probs[:, g[0], i // 2, (i % 2) * T:(i % 2 + 1) * T] if kt == 0 else
                                           probs[:, g[0], 2, i * P:(i + 1) * P])
                                    v = vst["L"][:, s, kt, half_, 4 * region + i, :]
                                    fin_ = half_ == 1 and kt == NT - 1
                                else:
                                    col, lead, q0 = 2 * half_ + i, kt == 0, 0
                                    src = probs[:, g[0], kt, i * T:(i + 1) * T]
                                    v = vst["F"][:, s, kt, 0, 4 * region + col, :]
                                    fin_ = kt == NT - 1
                                last = pe.matmul(pvp[32 * col:32 * col + 32, region * T + q0:(region + 1) * T], v, src,
                                                 start=lead, stop=fin_, skip_group_check=True,
                                                 tile_position=(0, 32 * col))
                        last.then_inc(q.b_pv, 1)
                    elif step == "ot":
                        pe.wait_ge(q.c_ost, u + 1)
                        transposes(mxp[:, OT_BANK, :], [ost[:, s, r, t * P:(t + 1) * P] for t in range(NT) for r in range(2)], q.c_ot)
                    elif step == "at":
                        pe.wait_ge(q.c_attn, u + 1)
                        dense_job(1, q.c_attnt, 1, off)
                        transposes(dense[1], [attn[:, s, t, :] for t in range(NT)], q.c_at)
                    elif step == "op":
                        if plan.causal:
                            pe.wait_ge(q.wc_ok, u + 1)
                        pe.wait_ge(q.c_attnt, u + 1)
                        dense_job(0, q.c_add, 1, off)
                        for t in range(NT):
                            last = pe.matmul(dense[0][:, t * D:(t + 1) * D], attnt[:, s, t * P:(t + 1) * P],
                                             wc[plan.name][:, C_O:C_O + D], start=True, stop=True)
                        last.then_inc(q.c_op, 1)
                    elif step == "xt2":
                        pe.wait_ge(q.c_xn2, u + 1)
                        dense_job(0, q.c_xn2t, 1, off)
                        transposes(dense[0], [xn[:, 1, s, t, :] for t in range(NT)], q.c_xt2)
                    elif step == "f1":
                        pe.wait_ge(q.c_xn2t, u + 1)
                        for k in range(2):
                            dense_job(k, q.c_gelu, NF, off)
                            for f in range(2 * k, 2 * k + 2):
                                last = pe.matmul(dense[k][:, (f % 2) * T:(f % 2 + 1) * T],
                                                 wc["L"][:, C_W1 + f * P:C_W1 + (f + 1) * P], xnt[:, 1, s, :],
                                                 start=True, stop=True)
                            last.then_inc(q.c_f1, 1)
                    elif step == "f2":
                        pe.wait_ge(q.c_gelu, NF * (u + 1))
                        dense_job(0, q.c_done, 1, off + BATCH)
                        for t in range(NT):
                            for f in range(NF):
                                last = pe.matmul(dense[0][:, t * D:(t + 1) * D], hid[:, s, f, t * P:(t + 1) * P],
                                                 wc["L"][:, C_W2 + f * D:C_W2 + (f + 1) * D], start=(f == 0),
                                                 stop=(f == NF - 1))
                        last.then_inc(q.c_f2, 1)

            def run(plan):
                read = [None, None]

                def body(n):
                    steps(plan, n, read)
                    for k in range(2):
                        if read[k] is not None:
                            before, per_round, constant = read[k]
                            read[k] = (before, per_round, constant - per_round)

                rounds_of(pe, plan, body)

            pe.wait_ge(s_init, 13)
            pe.wait_ge(s_initv, 1)
            pe.wait_ge(s_rounded, 6)
            pe.wait_ge(s_w, 16 * 5)
            run(EXPERT)
            pe.wait_ge(S["F"].c_done, BATCH)
            run(ENCODER)


def constant_rows():
    slopes = (2.0 ** -(2.0 ** -(np.log2(ENCODER.heads) - 3))) ** np.arange(1, ENCODER.heads + 1)
    slopes = slopes.astype(np.float32)
    bias = (slopes[:, None] * np.arange(T, dtype=np.float32)[None] / np.float32(ENCODER.scale)).astype(np.float32)
    high = (bias.view(np.uint32) & np.uint32(0xFFFFF000)).view(np.float32)
    low = bias - high
    n = P - ALIBI_ROW
    rq = np.zeros((n, GROUPS, ENCODER.hg, T), np.float32)
    rk = np.zeros((n, GROUPS, T), np.float32)
    for i in range(ENCODER.hg):
        for part, b in enumerate((high, low)):
            rq[2 * i + part, :, i, :] = 1.0
            rk[2 * i + part] = b[i::ENCODER.hg]
    rk[n - 1] = 1.0
    rkf = np.zeros((n, GROUPS, T), np.float32)
    rkf[n - 1] = 1.0
    return rq.reshape(n, -1), rk.reshape(n, -1), rkf.reshape(n, -1)


def segments():
    experts = 4
    keep = np.arange(D)[:, None] < (D // 2 ** (np.arange(T) // (T // experts)))[None]
    keep = keep.astype(np.float32)
    return keep, np.ascontiguousarray(keep.T.reshape(NT, P, D).transpose(1, 0, 2))


def kernel(**inputs):
    import concourse.bacc as bacc
    from concourse.bass_utils import run_bass_kernel_spmd

    g = {k: np.asarray(v) for k, v in inputs.items()}

    def rows(v):
        return np.broadcast_to(v[None], (P, v.shape[0]))

    head = np.arange(D).reshape(2, 2, 4, ENCODER.dh)
    v_order = head.transpose(1, 0, 2, 3).reshape(-1)
    o_order = head.transpose(0, 2, 1, 3).reshape(-1)
    def by_stack(plan):
        return np.arange(D).reshape(GROUPS, plan.hg, plan.dh).transpose(1, 2, 0).reshape(-1)

    order, order_f = by_stack(ENCODER), by_stack(EXPERT)
    wa, wc = [], []
    for l in range(LAYERS):
        w, b = g["L0_attn_in_proj_w"][l], g["L0_attn_in_proj_b"][l]
        wa.append(np.concatenate([
            w[0:D][order].T, w[D:2 * D][order].T, w[2 * D:][v_order].T, rows(b[2 * D:][v_order]),
            b[0:D][order][:, None], b[D:2 * D][order][:, None], g["L0_attn_ln1_w"][l][:, None], g["L0_attn_ln1_b"][l][:, None]], 1))
        w2 = g["L0_attn_ffn2_w"][l].T.reshape(NF, P, D).transpose(1, 0, 2).reshape(P, -1)
        wc.append(np.concatenate([
            g["L0_attn_out_proj_w"][l].T[o_order], rows(g["L0_attn_out_proj_b"][l]), g["L0_attn_ffn1_w"][l].T, w2,
            rows(g["L0_attn_ffn2_b"][l]), g["L0_attn_ln2_w"][l][:, None], g["L0_attn_ln2_b"][l][:, None],
            g["L0_attn_ffn1_b"][l].reshape(NF, P).T], 1))
    wa_f = np.concatenate([
        g["L0_ffn_q_w"][order_f].T, g["L0_ffn_k_w"][order_f].T, g["L0_ffn_v_w"].T, rows(g["L0_ffn_v_b"]),
        g["L0_ffn_q_b"][order_f][:, None], g["L0_ffn_k_b"][order_f][:, None], g["L0_ffn_norm_w"][:, None], g["L0_ffn_norm_b"][:, None]], 1)
    wc_f = np.concatenate([g["L0_ffn_o_w"].T, rows(g["L0_ffn_o_b"])], 1)
    fin = np.stack([rows(g["L0_attn_final_w"]), rows(g["L0_attn_final_b"])], 1)
    rq, rk, rkf = constant_rows()
    seg_in, seg_out = segments()
    named = {
        "x": g["L0_attn_x"], "wa_l": np.stack(wa), "wc_l": np.stack(wc), "wa_f": wa_f, "wc_f": wc_f, "fin": fin,
        "rows_q": rq, "rows_k": rk, "rows_kf": rkf, "seg_in": seg_in, "seg_out": seg_out}

    nc = bacc.Bacc("TRN2", target_bir_lowering=False, num_devices=1)
    arrays, args = {}, []
    for name, a in named.items():
        a = np.ascontiguousarray(a)
        arrays[f"in_{name}"] = a
        args.append(nc.dram_tensor(f"in_{name}", a.shape, mybir.dt.from_np(a.dtype), kind="ExternalInput").ap())
    result = nc.dram_tensor("out_0", (BATCH, T, D), F32, kind="ExternalOutput").ap()
    build(nc, *args, result)
    r = run_bass_kernel_spmd(nc, [arrays], core_ids=[0])
    return r.results[0]["out_0"]
```
